# Optimizing a Trainium2 kernel written in Bass

```python
import numpy as np
import jax
import jax.numpy as jnp

def _softmax(x, axis=-1):
    return jax.nn.softmax(x, axis=axis)

def _gelu(x):
    return jax.nn.gelu(x, approximate=True)

def _silu(x):
    return jax.nn.silu(x)

def _sigmoid(x):
    return jax.nn.sigmoid(x)

def _layernorm(x, axis=-1, eps=1e-05):
    m = jnp.mean(x, axis=axis, keepdims=True)
    v = jnp.var(x, axis=axis, keepdims=True)
    return (x - m) / jnp.sqrt(v + eps)

def _scatter_add(tgt, idx, src, axis=0):
    return tgt.at[idx].add(src)

def _segment_sum(src, seg, n):
    return jax.ops.segment_sum(src, seg, n)
kernel_name = 'mk_adj_preln_d2_adj_r2_777e24'

def setup_inputs(seed: int=0):
    np.random.seed(seed)
    _w = jnp.asarray

    def _rec_inputs():
        import jax
        import jax.numpy as jnp
        _gk = jax.random.key(seed)
        x = 7.22e-05 + 1 * jax.random.normal(jax.random.fold_in(_gk, 1), (128, 128, 512), jnp.float32)
        _w = (1.0 + jnp.arange(128, dtype=jnp.float32)) ** (-0.5)
        _w = _w / _w.mean()
        _pij = jnp.clip(0.125 * _w[:, None] * _w[None, :], 0.0, 1.0)
        _a = jax.random.uniform(jax.random.fold_in(_gk, 2), (128, 128)) < _pij
        _a = jnp.logical_or(_a, jnp.eye(128, dtype=bool))
        _af = _a.astype(jnp.float32)
        adj = _af
        return (x, adj)
    x, adj = _rec_inputs()

    def _L0_gnn_setup():
        import jax, jax.numpy as jnp
        import numpy as np
        EPS = 1e-08

        def _row_stochastic_causal(A, causal_mask):
            A = A * causal_mask
            deg = jnp.maximum(A.sum(axis=-1, keepdims=True), EPS)
            return A / deg
        key = jax.random.key(seed)
        k = jax.random.split(key, 5)
        B, N, D = (4, 1024, 512)
        s = 1.0 / np.sqrt(D)
        h = jax.random.normal(k[0], (B, N, D), dtype=jnp.float32)
        W_lang = jax.random.normal(k[1], (D, D), dtype=jnp.float32) * s
        W_grav = jax.random.normal(k[2], (D, D), dtype=jnp.float32) * s
        W_V = jax.random.normal(k[3], (D, D), dtype=jnp.float32) * s
        W_O = jax.random.normal(k[4], (D, D), dtype=jnp.float32) * s
        causal_mask = jnp.tril(jnp.ones((N, N), dtype=jnp.float32))
        gate_logit = jnp.zeros((), jnp.float32)
        log_sigma = jnp.zeros((), jnp.float32)
        return {'h': h, 'causal_mask': causal_mask, 'W_lang': W_lang, 'W_grav': W_grav, 'W_V': W_V, 'W_O': W_O, 'gate_logit': gate_logit, 'log_sigma': log_sigma}
    _L0_gnn_all = _L0_gnn_setup()
    _L0_gnn_in = {k: v for k, v in _L0_gnn_all.items() if k in ('W_lang', 'W_grav', 'W_V', 'W_O', 'gate_logit', 'log_sigma')}
    del _L0_gnn_all

    def _L1_gnn_setup():
        import jax, jax.numpy as jnp
        import numpy as np
        DIM = 199
        K_HOP = 3

        def _khop_support(n, k):
            A = np.eye(n, dtype=np.float64)
            idx = np.arange(n)
            A[idx, (idx + 1) % n] = 1.0
            A[(idx + 1) % n, idx] = 1.0
            S = np.linalg.matrix_power(A, k)
            return (S > 0).astype(np.float32)
        key = jax.random.key(seed)
        kx, kk = jax.random.split(key)
        batch, n, f = (128, DIM, 512)
        x = jax.random.normal(kx, (batch, n, f), dtype=jnp.float32)
        support = jnp.asarray(_khop_support(n, K_HOP))
        limit = float(np.sqrt(6.0 / (n + n)))
        kernel = jax.random.uniform(kk, (n, n), minval=-limit, maxval=limit, dtype=jnp.float32)
        bias = jnp.zeros((f,), dtype=jnp.float32)
        return {'x': x, 'support': support, 'kernel': kernel, 'bias': bias}
    _L1_gnn_all = _L1_gnn_setup()
    _L1_gnn_in = {k: v for k, v in _L1_gnn_all.items() if k in ('bias',)}
    del _L1_gnn_all
    return {'x': x, 'adj': adj, 'L0_gnn_W_lang': _L0_gnn_in['W_lang'], 'L0_gnn_W_grav': _L0_gnn_in['W_grav'], 'L0_gnn_W_V': _L0_gnn_in['W_V'], 'L0_gnn_W_O': _L0_gnn_in['W_O'], 'L0_gnn_gate_logit': _L0_gnn_in['gate_logit'], 'L0_gnn_log_sigma': _L0_gnn_in['log_sigma'], 'L1_gnn_bias': _L1_gnn_in['bias']}

def reference(x, adj, L0_gnn_W_lang, L0_gnn_W_grav, L0_gnn_W_V, L0_gnn_W_O, L0_gnn_gate_logit, L0_gnn_log_sigma, L1_gnn_bias):
    import jax
    import jax.numpy as jnp

    def _L0_gnn_ref(h, causal_mask, W_lang, W_grav, W_V, W_O, gate_logit, log_sigma):
        import jax, jax.numpy as jnp
        import numpy as np
        EPS = 1e-08

        def _row_stochastic_causal(A, causal_mask):
            A = A * causal_mask
            deg = jnp.maximum(A.sum(axis=-1, keepdims=True), EPS)
            return A / deg
        z_l = jnp.einsum('bnd,ed->bne', h, W_lang)
        z_g = jnp.einsum('bnd,ed->bne', h, W_grav)
        v = jnp.einsum('bnd,ed->bne', h, W_V)
        N = h.shape[-2]
        not_eye = 1.0 - jnp.eye(N, dtype=h.dtype)
        zn = z_l / jnp.maximum(jnp.linalg.norm(z_l, axis=-1, keepdims=True), EPS)
        A_l = jnp.maximum(jnp.einsum('bnd,bmd->bnm', zn, zn), 0.0) * not_eye
        sq = jnp.sum(z_g * z_g, axis=-1, keepdims=True)
        d2 = jnp.maximum(sq + jnp.swapaxes(sq, -1, -2) - 2.0 * jnp.einsum('bnd,bmd->bnm', z_g, z_g), 0.0)
        sigma = jnp.exp(log_sigma)
        A_g = jnp.exp(-d2 / (2.0 * sigma * sigma)) * not_eye
        K_l = _row_stochastic_causal(A_l, causal_mask)
        K_g = _row_stochastic_causal(A_g, causal_mask)
        w_l = jax.nn.sigmoid(gate_logit)
        K = w_l * K_l + (1.0 - w_l) * K_g
        out = jnp.einsum('bnm,bmd->bnd', K, v)
        return jnp.einsum('bnd,ed->bne', out, W_O)

    def _L1_gnn_ref(x, support, kernel, bias):
        import jax, jax.numpy as jnp
        import numpy as np
        DIM = 199
        K_HOP = 3

        def _khop_support(n, k):
            A = np.eye(n, dtype=np.float64)
            idx = np.arange(n)
            A[idx, (idx + 1) % n] = 1.0
            A[(idx + 1) % n, idx] = 1.0
            S = np.linalg.matrix_power(A, k)
            return (S > 0).astype(np.float32)
        W = support * kernel
        out = jnp.einsum('bnf,nm->bmf', x, W)
        out = out + bias
        return out
    h = jnp.maximum(_layernorm(x, axis=-1), 0.0)
    x = x + _L0_gnn_ref(h, adj, L0_gnn_W_lang, L0_gnn_W_grav, L0_gnn_W_V, L0_gnn_W_O, L0_gnn_gate_logit, L0_gnn_log_sigma)
    h = jnp.maximum(_layernorm(x, axis=-1), 0.0)
    x = x + _L1_gnn_ref(h, adj, adj, L1_gnn_bias)
    return x

_drawn_inputs = setup_inputs


def setup_inputs(seed=0):
    import zlib

    import numpy as np

    out = dict(_drawn_inputs(seed))
    spreads = {'L1_gnn_bias': (0.0, 0.69)}
    factors = {'L0_gnn_W_lang': 8.0}
    for name, (base, spread) in spreads.items():
        noise = np.random.default_rng([zlib.crc32(name.encode()), seed]).standard_normal(out[name].shape)
        drawn = base * np.exp(spread * noise) if base else spread * noise
        out[name] = jnp.asarray(drawn.astype(out[name].dtype))
    for name, factor in factors.items():
        out[name] = (out[name] * factor).astype(out[name].dtype)
    return out
```

```python
from contextlib import ExitStack

import concourse.bass as bass
from concourse import mybir

ALU = mybir.AluOpType
ACT = mybir.ActivationFunctionType
AX = mybir.AxisListType
F32 = mybir.dt.float32
F32R = mybir.dt.float32r

P = 128
GB = 4
SLOTS = 3
BANKS = 4
EPS_LN = 1e-5
EPS = 1e-8


def gnn_pair(nc, x, adj, w_lang, w_grav, w_v, w_o, gate_logit, log_sigma, bias, out):
    B, N, D = x.shape
    assert N == P and B % GB == 0 and D % P == 0 and D <= 512 and D // P == GB
    C = D // P
    NG = B // GB
    TRI = [(a, c) for a in range(C) for c in range(a + 1)]
    SUM, DIFF, SQ, DIFF4, VAR_IN, NEG_MEAN, VAR_BETWEEN, VAR, RSTD, SHIFT = range(10)
    LN_STEPS = 10
    RN_STEPS = 2
    blk = {ac: n for n, ac in enumerate(TRI)}

    G_USES = 2 * C
    SETUP = C + 2 * C + C
    PER = G_USES + GB + 2 * GB + GB

    def first_use(i):
        return GB + SETUP + PER * i

    HI_SETUP = 3 * C
    HI_PER = G_USES + 2 * GB

    def first_hi(i):
        return GB + HI_SETUP + HI_PER * i

    x_g = x.rearrange("(g b) n d -> g n b d", b=GB)
    out_g = out.rearrange("(g b) n d -> g b n d", b=GB)

    with ExitStack() as ctx:
        def sb(name, shape, dt=F32):
            return ctx.enter_context(nc.sbuf_tensor(name, shape, dt))

        def sem(name):
            return ctx.enter_context(nc.semaphore(name))

        x_ring = sb("x_ring", [P, SLOTS, GB, D])
        h = sb("h", [P, GB, D])
        hT = [sb(f"hT_{s}", [P, C, GB, P], F32R) for s in ("hi", "lo")]
        y = [sb(f"y_{s}", [P, C, GB, 2, P], F32R) for s in ("hi", "lo")]
        Lw = [sb(f"Lw_{s}", [P, 2, len(TRI), P], F32R) for s in ("hi", "lo")]
        MT = [sb(f"MT_{s}", [P, C, D], F32R) for s in ("hi", "lo")]
        v = [sb(f"v_{s}", [P, GB, D], F32R) for s in ("hi", "lo")]
        chain = sb("chain", [P, 3, GB, 2, P])
        P_sb, diag, A = (chain[:, n] for n in range(3))
        K = sb("K", [P, GB, P])
        KT = [sb(f"KT_{s}", [P, GB, P], F32R) for s in ("hi", "lo")]
        x2 = sb("x2", [P, GB, D])
        x_out = sb("x_out", [P, GB, D])
        h2f = sb("h2f", [P, GB, D])
        h2 = [sb(f"h2_{s}", [P, GB, D], F32R) for s in ("hi", "lo")]
        adj_sb = sb("adj_sb", [P, P])
        ident = sb("ident", [P, P])
        diag_of = sb("diag_of", [P, 2, P])
        off_diag = sb("off_diag", [P, P])
        mask = sb("mask", [P, P])
        adj2 = sb("adj2", [P, P])
        A2 = [sb(f"A2_{s}", [P, P], F32R) for s in ("hi", "lo")]
        bias_sb = sb("bias_sb", [P, D])
        scal = sb("scal", [P, 8])
        gate, lsig, w_l, w_g, egate, sig, sig2, inv_sig2 = (scal[:, n:n + 1] for n in range(8))
        w8 = sb("w8", [P, GB, 2])
        bn1 = sb("bn1", [P, GB, 6])
        bn2 = sb("bn2", [P, GB, 6])
        ln1 = sb("ln1", [P, LN_STEPS, GB])
        ln2 = sb("ln2", [P, LN_STEPS, GB])
        neg_half = sb("neg_half", [P, GB])
        quarter = sb("quarter", [P, GB])
        sq = sb("sq", [P, GB, 2])
        sqc = sb("sqc", [P, GB])
        rn = sb("rn", [P, GB, 2])
        wr = sb("wr", [P, GB, 2])
        deg = sb("deg", [P, 4, GB, 2])

        raw_l = x2[:, :, :]
        raw_g = h2f[:, :, :]
        raw_v = x_ring[:, SLOTS - 1]
        raw_o = chain[:, 0:2].rearrange("p a b l m -> p (a b l m)").rearrange("p (c n) -> p c n", c=C)
        w_oT = x_out[:, :, :]

        ring = ctx.enter_context(nc.psum_tensor("ring", [P, BANKS, 512], F32))
        p_ps = ctx.enter_context(nc.psum_tensor("p_ps", [P, GB, 2, P], F32))
        r_ps = ctx.enter_context(nc.psum_tensor("r_ps", [P, GB, P], F32))
        kt_ps = ctx.enter_context(nc.psum_tensor("kt_ps", [P, GB, P], F32))

        def bank(use):
            return ring[:, use % BANKS]

        x_loaded, consts_loaded = sem("x_loaded"), sem("consts_loaded")
        w_loaded = [sem(f"w_loaded_{s}") for s in ("lang", "grav", "o", "v")]
        out_stored = sem("out_stored")
        ident_set, ident_ready = sem("ident_set"), sem("ident_ready")
        exp_gate, scalars, weights_ready, a2_hi = sem("exp_gate"), sem("scalars"), sem("weights_ready"), sem("a2_hi")
        drained = sem("drained")
        hi_ready = sem("hi_ready")
        setup_mm = sem("setup_mm")
        t_done, g_done, p_done, v_done = sem("t_done"), sem("g_done"), sem("p_done"), sem("v_done")
        pt_done, r_done, kt_done, kv_done, l1_done = (
            sem("pt_done"), sem("r_done"), sem("kt_done"), sem("kv_done"), sem("l1_done"))
        h_ready = sem("h_ready")
        p_copied = sem("p_copied")
        exp_done = sem("exp_done")
        tg_ready = sem("tg_ready")
        kt_hi = sem("kt_hi")
        h2_hi = sem("h2_hi")
        bn1_done, bn2_done = sem("bn1_done"), sem("bn2_done")
        p_shifted = sem("p_shifted")
        s_ready = sem("s_ready")
        sq_ready = sem("sq_ready")
        a_ready = sem("a_ready")
        deg_step = sem("deg_step")
        k_ready = sem("k_ready")
        kt_split = sem("kt_split")
        h2_split = sem("h2_split")
        ln1_step, ln2_step = sem("ln1_step"), sem("ln2_step")
        h2_done = sem("h2_done")
        x2b_ready = sem("x2b_ready")
        diag_ready = sem("diag_ready")
        rn_step = sem("rn_step")

        def passes(hi_lo_lhs, hi_lo_rhs):
            return [(hi_lo_lhs[0], hi_lo_rhs[0]), (hi_lo_lhs[0], hi_lo_rhs[1]), (hi_lo_lhs[1], hi_lo_rhs[0])]

        def wait_for(eng, sem, count):
            if not isinstance(count, int) or count > 0:
                eng.wait_ge(sem, count)

        block = ctx.enter_context(nc.Block())

        @block.sync
        def _(sp):
            def load_x(g):
                sp.dma_start(x_ring[:, bass.ds(g % SLOTS, 1)].rearrange("p s b d -> p (s b) d"),
                             x_g[bass.ds(g, 1)].rearrange("g n b d -> (g n) b d")).then_inc(x_loaded, 16)

            def store_out(g, use):
                for b in range(GB):
                    sp.wait_ge(drained, use + b + 1)
                    sp.dma_start(out_g[bass.ds(g, 1), b].rearrange("g n d -> (g n) d"),
                                 x_out[:, b]).then_inc(out_stored, 16)

            def iteration(i, load=True, store=True, after=True):
                if load:
                    sp.wait_ge(x_loaded, 16 * i + 32)
                    sp.wait_ge(drained, first_use(i) + (G_USES + GB if store else 0))
                    load_x(i + 2)
                if store:
                    store_out(i - 1, first_use(i) + PER - GB * (1 if after else 2))

            for raw, w, loaded in ((raw_l, w_lang, w_loaded[0]), (raw_g, w_grav, w_loaded[1]),
                                   (raw_o, w_o, w_loaded[2]), (raw_v, w_v, w_loaded[3])):
                sp.dma_start(raw, w.rearrange("(c p) n -> p c n", p=P)).then_inc(loaded, 16)
            load_x(0)
            sp.wait_ge(x_loaded, 16)
            load_x(1)
            iteration(0, store=False)
            iteration(1)
            with sp.Fori(2, NG - 2) as i:
                iteration(i)
            iteration(NG - 2, load=False)
            iteration(NG - 1, load=False, after=False)
            store_out(NG - 1, first_use(NG))
            sp.wait_ge(out_stored, 16 * GB * NG)

        @block.gpsimd
        def _(pool):
            pool.memset(ident[:, :], 0.0).then_inc(ident_set, 1)
            pool.memset(diag_of[:, :, :], 0.0).then_inc(ident_set, 1)
            pool.memset(off_diag[:, :], 1.0).then_inc(ident_set, 1)
            pool.memset(neg_half[:, :], -0.5).then_inc(ident_set, 1)
            pool.memset(quarter[:, :], 0.25).then_inc(ident_set, 1)
            pool.memset(rn[:, :, :], 1.0).then_inc(ident_set, 1)
            pool.wait_ge(ident_set, 6)
            for m, fill in ((ident[:, :], 1.0), (diag_of[:, 0], 2.0), (diag_of[:, 1], -1.0), (off_diag[:, :], 0.0)):
                pool.affine_select(out=m, in_=m, compare_op=ALU.not_equal, fill=fill,
                                   base=0, pattern=[[-1, P]], channel_multiplier=1).then_inc(ident_ready, 1)

            def std_factors(g, bn, bn_done, t, step):
                pool.wait_ge(bn_done, GB * g + GB)
                pool.tensor_tensor(t[:, SUM], bn[:, :, 1], bn[:, :, 4], ALU.add).then_inc(step, 1)
                pool.tensor_tensor(t[:, DIFF], bn[:, :, 1], bn[:, :, 4], ALU.subtract).then_inc(step, 1)
                pool.tensor_tensor(t[:, SQ], bn[:, :, 2], bn[:, :, 5], ALU.add).then_inc(step, 1)
                pool.wait_ge(step, LN_STEPS * g + 3)
                pool.tensor_tensor(t[:, DIFF4], t[:, DIFF], quarter[:, :], ALU.mult).then_inc(step, 1)
                pool.tensor_scalar(t[:, VAR_IN], t[:, SQ], 1.0 / D, EPS_LN, ALU.mult, ALU.add).then_inc(step, 1)
                pool.tensor_scalar(t[:, NEG_MEAN], t[:, SUM], -0.5, None, ALU.mult).then_inc(step, 1)
                pool.wait_ge(step, LN_STEPS * g + 4)
                pool.tensor_tensor(t[:, VAR_BETWEEN], t[:, DIFF4], t[:, DIFF], ALU.mult).then_inc(step, 1)
                pool.wait_ge(step, LN_STEPS * g + 7)
                pool.tensor_tensor(t[:, VAR], t[:, VAR_BETWEEN], t[:, VAR_IN], ALU.add).then_inc(step, 1)
                pool.wait_ge(step, LN_STEPS * g + 8)
                pool.tensor_tensor(t[:, RSTD], t[:, VAR], neg_half[:, :], ALU.pow).then_inc(step, 1)
                pool.wait_ge(step, LN_STEPS * g + 9)
                pool.tensor_tensor(t[:, SHIFT], t[:, NEG_MEAN], t[:, RSTD], ALU.mult).then_inc(step, 1)

            def norm1(g):
                wait_for(pool, h_ready, GB * g)
                std_factors(g, bn1, bn1_done, ln1, ln1_step)

            def add_bias(g, b):
                if b == 0:
                    wait_for(pool, out_stored, 16 * GB * g)
                pool.wait_ge(bn2_done, GB * g + b + 1)
                pool.tensor_tensor(x_out[:, b], x2[:, b], bias_sb[:, :], ALU.add).then_inc(x2b_ready, 1)

            def norm2(g):
                std_factors(g, bn2, bn2_done, ln2, ln2_step)

            def h2_lo(g, b):
                pool.wait_ge(h2_hi, GB * g + b + 1)
                pool.tensor_tensor(h2[1][:, b], h2f[:, b], h2[0][:, b].bitcast(F32), ALU.subtract)\
                    .then_inc(h2_split, 1)

            def diagonal(g):
                pool.wait_ge(p_copied, 2 * g + 2)
                wait_for(pool, sq_ready, 2 * g)
                select = diag_of[:, :, :].rearrange("p l m -> p (l m)").unsqueeze(1).to_broadcast([P, GB, 2 * P])
                pool.tensor_tensor(diag.rearrange("p b l m -> p b (l m)"),
                                   P_sb.rearrange("p b l m -> p b (l m)"), select, ALU.mult).then_inc(diag_ready, 1)

            def row_norms(g):
                pool.wait_ge(sq_ready, 2 * g + 2)
                wait_for(pool, k_ready, g)
                pool.tensor_tensor(rn[:, :, 0], sqc[:, :], neg_half[:, :], ALU.pow).then_inc(rn_step, 1)
                pool.wait_ge(rn_step, RN_STEPS * g + 1)
                pool.tensor_tensor(wr[:, :, :], rn[:, :, :], w8[:, :, :], ALU.mult).then_inc(rn_step, 1)

            def iteration(i, before=True, after=True):
                if after:
                    norm1(i + 1)
                if before:
                    for b in range(GB // 2):
                        add_bias(i - 1, b)
                    norm2(i - 1)
                diagonal(i)
                if before:
                    for b in range(GB // 2, GB):
                        add_bias(i - 1, b)
                row_norms(i)
                if before:
                    for b in range(GB):
                        h2_lo(i - 1, b)

            norm1(0)
            pool.wait_ge(scalars, 9)
            pool.wait_ge(consts_loaded, 16 * 4)
            iteration(0, before=False)
            iteration(1)
            with pool.Fori(2, NG - 1) as i:
                iteration(i)
            iteration(NG - 1, after=False)
            norm2(NG - 1)
            for b in range(GB):
                h2_lo(NG - 1, b)
            for b in range(GB):
                add_bias(NG - 1, b)

        @block.scalar
        def _(act):
            act.dma_start(gate, gate_logit.unsqueeze(0).to_broadcast([P, 1])).then_inc(consts_loaded, 16)
            act.dma_start(lsig, log_sigma.unsqueeze(0).to_broadcast([P, 1])).then_inc(consts_loaded, 16)
            act.dma_start(adj_sb[:, :], adj).then_inc(consts_loaded, 16)
            act.dma_start(bias_sb[:, :], bias.unsqueeze(0).to_broadcast([P, D])).then_inc(consts_loaded, 16)

            def apply_norm1(g, wait_free=True):
                act.wait_ge(ln1_step, LN_STEPS * (g + 1))
                if wait_free:
                    act.wait_ge(t_done, GB * g)
                for b in range(GB):
                    xb = x_ring[:, bass.ds(g % SLOTS, 1), b].rearrange("p s d -> p (s d)")
                    act.activation(h[:, b], xb, ACT.Relu, bias=ln1[:, SHIFT, b:b + 1],
                                   scale=ln1[:, RSTD, b:b + 1]).then_inc(h_ready, 1)

            def t_hi(g, b, n):
                act.wait_ge(t_done, GB * g + b + 1)
                act.activation(hT[0][:, :, b], bank(n).rearrange("p (c m) -> p c m", c=C), ACT.Copy)\
                   .then_inc(hi_ready, 1)

            def iteration(i, before=True, after=True):
                n = 0
                if before:
                    act.wait_ge(p_done, GB * i)
                for a in range(C):
                    for l in range(2):
                        act.wait_ge(g_done, G_USES * i + n + 1)
                        act.activation(y[0][:, a, :, l], bank(n).rearrange("p (b m) -> p b m", b=GB), ACT.Copy)\
                           .then_inc(hi_ready, 1)
                        n += 1
                        if before and n == 4:
                            w_g_K_g(i - 1)
                        if before and n == G_USES - 1:
                            kt_copy(i - 1)
                n += GB
                if after:
                    apply_norm1(i + 1)
                if before:
                    act.wait_ge(s_ready, i)
                    act.wait_ge(diag_ready, i)
                for half in range(2):
                    act.wait_ge(p_done, GB * i + 2 * half + 2)
                    act.activation(P_sb[:, 2 * half:2 * half + 2], p_ps[:, 2 * half:2 * half + 2], ACT.Copy)\
                       .then_inc(p_copied, 1)
                if before:
                    h2_full(i - 1, 0)
                    h2_full(i - 1, 1)
                    act.wait_ge(kv_done, GB * i)
                for b in range(GB):
                    act.wait_ge(v_done, GB * i + b + 1)
                    act.activation(v[0][:, b], bank(n), ACT.Copy).then_inc(hi_ready, 1)
                    n += 1
                    if after:
                        t_hi(i + 1, b, n)
                        n += 1
                    if before and b < 3:
                        for q in range(2 * b, 2 * b + 2):
                            (h2_full if b == 0 else h2_copy)(i - 1, q + 2 if b == 0 else q - 2)
                    if b == 0:
                        shift(i)
                exponentials(i)

            def h2_full(g, b):
                if b == 0:
                    act.wait_ge(ln2_step, LN_STEPS * (g + 1))
                    wait_for(act, h2_split, GB * g)
                act.activation(h2f[:, b], x2[:, b], ACT.Relu, bias=ln2[:, SHIFT, b:b + 1],
                               scale=ln2[:, RSTD, b:b + 1]).then_inc(h2_done, 1)

            def h2_copy(g, b):
                act.wait_ge(h2_done, GB * g + b + 1)
                if b == 0:
                    wait_for(act, l1_done, GB * g)
                act.activation(h2[0][:, b], h2f[:, b], ACT.Copy).then_inc(h2_hi, 1)

            def shift(g):
                act.wait_ge(sq_ready, 2 * g + 1)
                for b in range(GB):
                    e = act.activation(P_sb[:, b, 1], P_sb[:, b, 1], ACT.Identity, bias=sq[:, b, 1:2])
                e.then_inc(p_shifted, 1)

            def exponentials(g):
                act.wait_ge(s_ready, g + 1)
                act.activation(A[:, :, 1], A[:, :, 1], ACT.Exp, scale=inv_sig2).then_inc(exp_done, 1)

            def w_g_K_g(g):
                act.wait_ge(deg_step, 5 * g + 5)
                wait_for(act, kt_done, g)
                for b in range(GB):
                    e = act.activation(K[:, b], A[:, b, 1], ACT.Copy, scale=deg[:, 3, b, 1:2])
                e.then_inc(tg_ready, 1)

            def kt_copy(g):
                act.wait_ge(kt_done, g + 1)
                wait_for(act, kv_done, GB * g)
                act.activation(KT[0][:, :, :], kt_ps[:, :, :], ACT.Copy).then_inc(kt_hi, 1)

            act.wait_ge(consts_loaded, 16 * 4)
            act.activation(egate, gate, ACT.Exp, scale=-1.0).then_inc(exp_gate, 1)
            act.activation(sig, lsig, ACT.Exp).then_inc(exp_gate, 1)
            use = 0
            for l in range(2):
                for c in range(C):
                    act.wait_ge(setup_mm, use + 1)
                    for a in range(c, C):
                        e = act.activation(Lw[0][:, l, blk[a, c]], bank(use)[:, (a - c) * P:(a - c + 1) * P],
                                           ACT.Copy, scale=0.5 if a == c else 1.0)
                    e.then_inc(hi_ready, 1)
                    use += 1
            act.wait_ge(weights_ready, 1)
            act.activation(A2[0][:, :], adj2[:, :], ACT.Copy).then_inc(a2_hi, 1)
            apply_norm1(0, wait_free=False)
            use += C
            for c in range(C):
                act.wait_ge(setup_mm, use + 1)
                act.activation(MT[0][:, c], bank(use), ACT.Copy).then_inc(hi_ready, 1)
                use += 1
            for b in range(GB):
                t_hi(0, b, use + b)
            iteration(0, before=False)
            iteration(1)
            with act.Fori(2, NG - 1) as i:
                iteration(i)
            iteration(NG - 1, after=False)
            w_g_K_g(NG - 1)
            kt_copy(NG - 1)
            for b in range(GB):
                h2_full(NG - 1, b)
                if b:
                    h2_copy(NG - 1, b - 1)
            h2_copy(NG - 1, GB - 1)

        @block.vector
        def _(dve):
            def part(t):
                return t.bitcast(F32)

            def lo(out, ps, hi, n_hi, scale=None):
                dve.wait_ge(hi_ready, n_hi)
                if scale is None:
                    return dve.tensor_tensor(out, ps, part(hi), ALU.subtract)
                return dve.scalar_tensor_tensor(out=out, in0=ps, scalar=scale, in1=part(hi),
                                                op0=ALU.mult, op1=ALU.subtract)

            def t_lo(b, n, n_hi):
                return lo(hT[1][:, :, b], bank(n).rearrange("p (c m) -> p c m", c=C), hT[0][:, :, b], n_hi)

            def x_stats(g):
                dve.wait_ge(x_loaded, 16 * g + 16)
                wait_for(dve, ln1_step, LN_STEPS * g)
                for b in range(GB):
                    xb = x_ring[:, bass.ds(g % SLOTS, 1), b].rearrange("p s d -> p (s d)")
                    dve.bn_stats(bn1[:, b], xb).then_inc(bn1_done, 1)

            def similarities(g):
                dve.wait_ge(r_done, g + 1)
                dve.wait_ge(s_ready, g + 1)
                dve.tensor_tensor(A[:, :, 0], A[:, :, 0], r_ps[:, :, :], ALU.mult).then_inc(a_ready, 1)

            maskb = mask[:, :].unsqueeze(1).to_broadcast([P, GB, P])

            def mask_l(g):
                dve.wait_ge(a_ready, 3 * g + 1)
                dve.scalar_tensor_tensor(out=A[:, :, 0], in0=A[:, :, 0], scalar=0.0, in1=maskb,
                                         op0=ALU.max, op1=ALU.mult).then_inc(a_ready, 1)

            def mask_g(g):
                dve.wait_ge(exp_done, g + 1)
                dve.scalar_tensor_tensor(out=A[:, :, 1], in0=A[:, :, 1], scalar=1.0, in1=maskb,
                                         op0=ALU.min, op1=ALU.mult).then_inc(a_ready, 1)

            def row_factors(g):
                dve.wait_ge(a_ready, 3 * g + 3)
                dve.tensor_reduce(deg[:, 0], A, AX.X, ALU.add).then_inc(deg_step, 1)
                dve.wait_ge(deg_step, 5 * g + 1)
                dve.tensor_tensor(deg[:, 1], deg[:, 0], rn[:, :, :], ALU.mult).then_inc(deg_step, 1)
                dve.wait_ge(deg_step, 5 * g + 2)
                dve.tensor_scalar(deg[:, 1], deg[:, 1], EPS, None, ALU.max).then_inc(deg_step, 1)
                dve.wait_ge(deg_step, 5 * g + 3)
                dve.reciprocal(deg[:, 2], deg[:, 1]).then_inc(deg_step, 1)
                dve.wait_ge(deg_step, 5 * g + 4)
                dve.tensor_tensor(deg[:, 3], deg[:, 2], wr[:, :, :], ALU.mult).then_inc(deg_step, 1)

            def combine(g):
                dve.wait_ge(tg_ready, g + 1)
                for b in range(GB):
                    e = dve.scalar_tensor_tensor(out=K[:, b], in0=A[:, b, 0], scalar=deg[:, 3, b, 0:1],
                                                 in1=K[:, b], op0=ALU.mult, op1=ALU.add)
                e.then_inc(k_ready, 1)

            def kt_lo(g):
                dve.wait_ge(kt_hi, g + 1)
                dve.tensor_tensor(KT[1][:, :, :], kt_ps[:, :, :], part(KT[0][:, :, :]), ALU.subtract).then_inc(kt_split, 1)

            def residual(g, n, use):
                wait_for(dve, h2_done, GB * g)
                wait_for(dve, x2b_ready, GB * g)

                def add(b):
                    xb = x_ring[:, bass.ds(g % SLOTS, 1), b].rearrange("p s d -> p (s d)")
                    dve.wait_ge(kv_done, GB * g + b + 1)
                    dve.tensor_tensor(x2[:, b], bank(n + b), xb, ALU.add).then_inc(drained, 1)

                def stats(b):
                    dve.wait_ge(drained, use + b + 1)
                    dve.bn_stats(bn2[:, b], x2[:, b]).then_inc(bn2_done, 1)

                add(0)
                for b in range(1, GB):
                    add(b)
                    stats(b - 1)
                stats(GB - 1)

            def output(g, b, n):
                dve.wait_ge(l1_done, GB * g + b + 1)
                dve.wait_ge(x2b_ready, GB * g + b + 1)
                dve.tensor_tensor(x_out[:, b], bank(n), x_out[:, b], ALU.add).then_inc(drained, 1)

            def iteration(i, before=True, after=True):
                n = 0
                hi = first_hi(i)
                for a in range(C):
                    for l in range(2):
                        hi = hi + 1
                        lo(y[1][:, a, :, l], bank(n).rearrange("p (b m) -> p b m", b=GB), y[0][:, a, :, l], hi)\
                            .then_inc(drained, 1 if before or n < G_USES - 1 else 1 + GB)
                        n += 1
                        if before and n == 1:
                            mask_g(i - 1)
                        if before and n == 2:
                            row_factors(i - 1)
                        if before and n == 4:
                            combine(i - 1)
                        if after and n == 6:
                            x_stats(i + 1)
                        if before and n == G_USES - 1:
                            kt_lo(i - 1)
                if before:
                    residual(i - 1, n, first_use(i) + n)
                n += GB
                for b in range(GB):
                    hi = hi + 1
                    lo(v[1][:, b], bank(n), v[0][:, b], hi).then_inc(drained, 1)
                    n += 1
                    if after:
                        hi = hi + 1
                        t_lo(b, n, hi).then_inc(drained, 1 if before or b < GB - 1 else 1 + GB)
                        n += 1
                    if b == 0:
                        dve.wait_ge(diag_ready, i + 1)
                        wait_for(dve, rn_step, RN_STEPS * i)
                        wait_for(dve, p_shifted, i)
                        dve.tensor_reduce(sq[:, :, :], diag, AX.X, ALU.add).then_inc(sq_ready, 1)
                        dve.wait_ge(sq_ready, 2 * i + 1)
                        dve.tensor_scalar(sqc[:, :], sq[:, :, 0], EPS * EPS, None, ALU.max).then_inc(sq_ready, 1)
                    if b == 2:
                        dve.wait_ge(pt_done, i + 1)
                        dve.tensor_tensor(A, p_ps[:, :, :, :], P_sb, ALU.add).then_inc(s_ready, 1)
                if before:
                    output(i - 1, 0, n)
                    n += 1
                if before:
                    output(i - 1, 1, n)
                    output(i - 1, 2, n + 1)
                similarities(i)
                if before:
                    output(i - 1, 3, n + 2)
                mask_l(i)

            dve.wait_ge(ident_ready, 4)
            dve.wait_ge(consts_loaded, 16 * 4)
            dve.tensor_tensor(mask[:, :], adj_sb[:, :], off_diag[:, :], ALU.mult)
            dve.tensor_tensor(adj2[:, :], adj_sb[:, :], adj_sb[:, :], ALU.mult).then_inc(weights_ready, 1)
            dve.wait_ge(exp_gate, 2)
            dve.tensor_scalar(w_l, egate, 1.0, None, ALU.add).then_inc(scalars, 1)
            dve.tensor_tensor(sig2, sig, sig, ALU.mult).then_inc(scalars, 1)
            dve.wait_ge(scalars, 2)
            dve.reciprocal(w_l, w_l).then_inc(scalars, 1)
            dve.reciprocal(inv_sig2, sig2).then_inc(scalars, 1)
            dve.wait_ge(scalars, 4)
            dve.tensor_scalar(w_g, w_l, -1.0, 1.0, ALU.mult, ALU.add).then_inc(scalars, 1)
            dve.wait_ge(scalars, 5)
            for b in range(GB):
                dve.tensor_copy(w8[:, b], scal[:, 2:4]).then_inc(scalars, 1)
            use, hi = 0, 0
            for l in range(2):
                for c in range(C):
                    hi += 1
                    for a in range(c, C):
                        e = lo(Lw[1][:, l, blk[a, c]], bank(use)[:, (a - c) * P:(a - c + 1) * P],
                               Lw[0][:, l, blk[a, c]], hi, 0.5 if a == c else 1.0)
                    e.then_inc(drained, 1)
                    use += 1
            for c in range(C):
                dve.wait_ge(setup_mm, use + 1)
                dve.tensor_copy(w_oT[:, c], bank(use)).then_inc(drained, 1)
                use += 1
            x_stats(0)
            for c in range(C):
                hi += 1
                lo(MT[1][:, c], bank(use), MT[0][:, c], hi).then_inc(drained, 1)
                use += 1
            dve.wait_ge(a2_hi, 1)
            dve.tensor_tensor(A2[1][:, :], adj2[:, :], part(A2[0][:, :]), ALU.subtract).then_inc(weights_ready, 1)
            for b in range(GB):
                hi += 1
                t_lo(b, use + b, hi).then_inc(drained, 1)

            iteration(0, before=False)
            iteration(1)
            with dve.Fori(2, NG - 1) as i:
                iteration(i)
            iteration(NG - 1, after=False)
            g = NG - 1
            mask_g(g)
            row_factors(g)
            combine(g)
            kt_lo(g)
            use = first_use(g) + PER - GB
            residual(g, 0, use)
            for b in range(GB):
                output(g, b, b)

        @block.tensor
        def _(pe):
            def free(use):
                wait_for(pe, drained, use - BANKS + 1)

            def transposes_h(g, b, n, use):
                pe.wait_ge(h_ready, GB * g + b + 1)
                free(use)
                for c in range(C):
                    mm = pe.transpose(bank(n)[:, c * P:(c + 1) * P], h[:, b, c * P:(c + 1) * P], ident[:, :])
                mm.then_inc(t_done, 1)

            def product(out, terms):
                for k, (lhsT, rhs) in enumerate(terms):
                    mm = pe.matmul(out, lhsT, rhs, start=(k == 0), stop=(k == len(terms) - 1))
                return mm

            def y_block(a, l, n, use):
                free(use)
                product(bank(n), [t for c in range(a + 1) for t in passes(
                    [w[:, l, blk[a, c]] for w in Lw],
                    [w[:, c].rearrange("p b m -> p (b m)") for w in hT])]).then_inc(g_done, 1)

            def transposes_K(g):
                pe.wait_ge(k_ready, g + 1)
                for b in range(GB):
                    mm = pe.transpose(kt_ps[:, b], K[:, b], ident[:, :])
                mm.then_inc(kt_done, 1)

            def k_v(g, b, n, use):
                free(use)
                product(bank(n), passes([w[:, b] for w in KT], [w[:, b] for w in v])).then_inc(kv_done, 1)

            def layer1(g, b, n, use):
                pe.wait_ge(h2_split, GB * g + b + 1)
                free(use)
                product(bank(n), passes([w[:, :] for w in A2], [w[:, b] for w in h2])).then_inc(l1_done, 1)

            def iteration(i, before=True, after=True):
                n, use = 0, first_use(i)
                for a in range(C):
                    for l in range(2):
                        y_block(a, l, n, use + n)
                        n += 1
                        if before and n == G_USES - 1:
                            transposes_K(i - 1)
                if before:
                    pe.wait_ge(kt_split, i)
                    for b in range(GB):
                        k_v(i - 1, b, n + b, use + n + b)
                n += GB
                pe.wait_ge(drained, use + G_USES)
                for b in range(GB):
                    product(p_ps[:, b].rearrange("p l m -> p (l m)"), [t for a in range(C) for t in passes(
                        [w[:, a, b] for w in hT],
                        [w[:, a, b].rearrange("p l m -> p (l m)") for w in y])]).then_inc(p_done, 1)
                for b in range(GB):
                    free(use + n)
                    product(bank(n), [t for c in range(C) for t in passes(
                        [w[:, c, b] for w in hT], [w[:, c] for w in MT])]).then_inc(v_done, 1)
                    n += 1
                    if b == 2:
                        pe.wait_ge(p_shifted, i + 1)
                        for k in range(2 * GB):
                            mm = pe.transpose(p_ps[:, k // 2, k % 2], P_sb[:, k // 2, k % 2], ident[:, :])
                        mm.then_inc(pt_done, 1)
                    if after:
                        transposes_h(i + 1, b, n, use + n)
                        n += 1
                pe.wait_ge(rn_step, RN_STEPS * (i + 1))
                for b in range(GB):
                    mm = pe.transpose(r_ps[:, b], rn[:, b, 0:1].to_broadcast([P, P]), ident[:, :])
                mm.then_inc(r_done, 1)
                if before:
                    for b in range(GB):
                        layer1(i - 1, b, n + b, use + n + b)

            use = 0
            for l, raw in enumerate((raw_l, raw_g)):
                pe.wait_ge(w_loaded[l], 16)
                for c in range(C):
                    free(use)
                    product(bank(use)[:, 0:D - c * P],
                            [(raw[:, e, c * P:(c + 1) * P], raw[:, e, c * P:D]) for e in range(C)])\
                        .then_inc(setup_mm, 1)
                    use += 1
            pe.wait_ge(w_loaded[2], 16)
            pe.wait_ge(ident_ready, 4)
            for c in range(C):
                free(use)
                for r in range(C):
                    mm = pe.transpose(bank(use)[:, r * P:(r + 1) * P], raw_o[:, r, c * P:(c + 1) * P], ident[:, :])
                mm.then_inc(setup_mm, 1)
                use += 1
            pe.wait_ge(w_loaded[3], 16)
            pe.wait_ge(drained, use)
            for c in range(C):
                free(use)
                product(bank(use), [(raw_v[:, e, c * P:(c + 1) * P], w_oT[:, e]) for e in range(C)])\
                    .then_inc(setup_mm, 1)
                use += 1
            for b in range(GB):
                transposes_h(0, b, use, use)
                use += 1
            pe.wait_ge(drained, use)
            pe.wait_ge(weights_ready, 2)

            iteration(0, before=False)
            iteration(1)
            with pe.Fori(2, NG - 1) as i:
                iteration(i)
            iteration(NG - 1, after=False)
            g = NG - 1
            use = first_use(g) + PER - GB
            transposes_K(g)
            pe.wait_ge(kt_split, NG)
            for b in range(GB):
                k_v(g, b, b, use + b)
            for b in range(GB):
                layer1(g, b, b, use + GB + b)


_INS = ["x", "adj", "L0_gnn_W_lang", "L0_gnn_W_grav", "L0_gnn_W_V", "L0_gnn_W_O",
        "L0_gnn_gate_logit", "L0_gnn_log_sigma", "L1_gnn_bias"]


def kernel(**inputs):
    import numpy as np
    import concourse.bacc as bacc
    from concourse.bass_utils import run_bass_kernel_spmd

    nc = bacc.Bacc("TRN2", target_bir_lowering=False, num_devices=1)
    arrays, args = {}, []
    for name in _INS:
        a = np.ascontiguousarray(inputs[name])
        if a.ndim == 0:
            a = a.reshape(1)
        arrays[f"in_{name}"] = a
        args.append(nc.dram_tensor(f"in_{name}", a.shape, mybir.dt.from_np(a.dtype), kind="ExternalInput").ap())
    out = nc.dram_tensor("out", arrays["in_x"].shape, F32, kind="ExternalOutput").ap()
    gnn_pair(nc, *args, out)
    r = run_bass_kernel_spmd(nc, [arrays], core_ids=[0])
    return r.results[0]["out"]
```

```python
from contextlib import ExitStack

import concourse.bass as bass
from concourse import mybir

ALU = mybir.AluOpType
ACT = mybir.ActivationFunctionType
AX = mybir.AxisListType
F32 = mybir.dt.float32
F32R = mybir.dt.float32r

P = 128
GB = 4
SLOTS = 3
BANKS = 4
EPS_LN = 1e-5
EPS = 1e-8


def gnn_pair(nc, x, adj, w_lang, w_grav, w_v, w_o, gate_logit, log_sigma, bias, out):
    B, N, D = x.shape
    assert N == P and B % GB == 0 and D % P == 0 and D <= 512 and D // P == GB
    C = D // P
    NG = B // GB
    TRI = [(a, c) for a in range(C) for c in range(a + 1)]
    SUM, DIFF, SQ, DIFF4, VAR_IN, NEG_MEAN, VAR_BETWEEN, VAR, RSTD, SHIFT = range(10)
    LN_STEPS = 10
    RN_STEPS = 2
    blk = {ac: n for n, ac in enumerate(TRI)}

    G_USES = 2 * C
    SETUP = 2 * C + C
    PER = G_USES + GB + 2 * GB + GB

    def first_use(i):
        return SETUP + GB + PER * i

    HI_PER = G_USES + 2 * GB

    def first_hi(i):
        return SETUP + GB + HI_PER * i + (C if not isinstance(i, int) or i else 0)

    x_g = x.rearrange("(g b) n d -> g n b d", b=GB)
    out_g = out.rearrange("(g b) n d -> g b n d", b=GB)

    with ExitStack() as ctx:
        def sb(name, shape, dt=F32):
            return ctx.enter_context(nc.sbuf_tensor(name, shape, dt))

        def sem(name):
            return ctx.enter_context(nc.semaphore(name))

        x_ring = sb("x_ring", [P, SLOTS, GB, D])
        h = sb("h", [P, GB, D])
        hT = [sb(f"hT_{s}", [P, C, GB, P], F32R) for s in ("hi", "lo")]
        y = [sb(f"y_{s}", [P, C, GB, 2, P], F32R) for s in ("hi", "lo")]
        Lw = [sb(f"Lw_{s}", [P, 2, len(TRI), P], F32R) for s in ("hi", "lo")]
        MT = [sb(f"MT_{s}", [P, C, D], F32R) for s in ("hi", "lo")]
        v = [sb(f"v_{s}", [P, GB, D], F32R) for s in ("hi", "lo")]
        chain = sb("chain", [P, 3, GB, 2, P])
        P_sb, diag, A = (chain[:, n] for n in range(3))
        K = sb("K", [P, GB, P])
        KT = [sb(f"KT_{s}", [P, GB, P], F32R) for s in ("hi", "lo")]
        x2 = sb("x2", [P, GB, D])
        x_out = sb("x_out", [P, GB, D])
        h2f = sb("h2f", [P, GB, D])
        h2 = [sb(f"h2_{s}", [P, GB, D], F32R) for s in ("hi", "lo")]
        adj_sb = sb("adj_sb", [P, P])
        ident = sb("ident", [P, P])
        diag_of = sb("diag_of", [P, 2, P])
        off_diag = sb("off_diag", [P, P])
        mask = sb("mask", [P, P])
        adj2 = sb("adj2", [P, P])
        A2 = [sb(f"A2_{s}", [P, P], F32R) for s in ("hi", "lo")]
        bias_sb = sb("bias_sb", [P, D])
        scal = sb("scal", [P, 8])
        gate, lsig, w_l, w_g, egate, sig, sig2, inv_sig2 = (scal[:, n:n + 1] for n in range(8))
        w8 = sb("w8", [P, GB, 2])
        bn1 = sb("bn1", [P, GB, 6])
        bn2 = sb("bn2", [P, GB, 6])
        ln1 = sb("ln1", [P, LN_STEPS, GB])
        ln2 = sb("ln2", [P, LN_STEPS, GB])
        neg_half = sb("neg_half", [P, GB])
        quarter = sb("quarter", [P, GB])
        sq = sb("sq", [P, GB, 2])
        sqc = sb("sqc", [P, GB])
        rn = sb("rn", [P, GB, 2])
        wr = sb("wr", [P, GB, 2])
        deg = sb("deg", [P, 4, GB, 2])

        raw_l = x2[:, :, :]
        raw_g = h2f[:, :, :]
        raw_v = x_ring[:, SLOTS - 1]
        raw_o = chain[:, 0:2].rearrange("p a b l m -> p (a b l m)").rearrange("p (c n) -> p c n", c=C)
        y_rows = [w[:, :, :, :, :].rearrange("p c b l m -> p (c b l m)").rearrange("p (q n) -> p q n", n=D)
                  for w in y]
        wl_parts = [w[:, 0:C] for w in y_rows]
        wg_parts = [w[:, C:2 * C] for w in y_rows]
        wv_parts = [w[:, :, :] for w in v]
        woT_parts = [w[:, :, :] for w in h2]

        ring = ctx.enter_context(nc.psum_tensor("ring", [P, BANKS, 512], F32))
        p_ps = ctx.enter_context(nc.psum_tensor("p_ps", [P, GB, 2, P], F32))
        r_ps = ctx.enter_context(nc.psum_tensor("r_ps", [P, GB, P], F32))
        kt_ps = ctx.enter_context(nc.psum_tensor("kt_ps", [P, GB, P], F32))

        def bank(use):
            return ring[:, use % BANKS]

        x_loaded, consts_loaded = sem("x_loaded"), sem("consts_loaded")
        w_loaded = {s: sem(f"w_loaded_{s}") for s in ("l0", "l1", "l2", "l3", "g", "o", "v")}
        w_hi, w_split = sem("w_hi"), sem("w_split")
        out_stored = sem("out_stored")
        ident_set, ident_ready = sem("ident_set"), sem("ident_ready")
        exp_gate, scalars, a2_step, a2_hi = sem("exp_gate"), sem("scalars"), sem("a2_step"), sem("a2_hi")
        drained = sem("drained")
        hi_ready = sem("hi_ready")
        setup_mm = sem("setup_mm")
        t_done, g_done, p_done, v_done = sem("t_done"), sem("g_done"), sem("p_done"), sem("v_done")
        pt_done, r_done, kt_done, kv_done, l1_done = (
            sem("pt_done"), sem("r_done"), sem("kt_done"), sem("kv_done"), sem("l1_done"))
        h_ready = sem("h_ready")
        p_copied = sem("p_copied")
        exp_done = sem("exp_done")
        tg_ready = sem("tg_ready")
        kt_hi = sem("kt_hi")
        h2_hi = sem("h2_hi")
        bn1_done, bn2_done = sem("bn1_done"), sem("bn2_done")
        p_shifted = sem("p_shifted")
        s_ready = sem("s_ready")
        sq_ready = sem("sq_ready")
        a_ready = sem("a_ready")
        deg_step = sem("deg_step")
        k_ready = sem("k_ready")
        kt_split = sem("kt_split")
        h2_split = sem("h2_split")
        ln1_step, ln2_step = sem("ln1_step"), sem("ln2_step")
        h2_done = sem("h2_done")
        x2b_ready = sem("x2b_ready")
        diag_ready = sem("diag_ready")
        rn_step = sem("rn_step")

        def passes(hi_lo_lhs, hi_lo_rhs):
            return [(hi_lo_lhs[0], hi_lo_rhs[0]), (hi_lo_lhs[0], hi_lo_rhs[1]), (hi_lo_lhs[1], hi_lo_rhs[0])]

        def wait_for(eng, sem, count):
            if not isinstance(count, int) or count > 0:
                eng.wait_ge(sem, count)

        block = ctx.enter_context(nc.Block())

        @block.sync
        def _(sp):
            def load_x(g):
                sp.dma_start(x_ring[:, bass.ds(g % SLOTS, 1)].rearrange("p s b d -> p (s b) d"),
                             x_g[bass.ds(g, 1)].rearrange("g n b d -> (g n) b d")).then_inc(x_loaded, 16)

            def store_out(g, use):
                for b in range(GB):
                    sp.wait_ge(drained, use + b + 1)
                    sp.dma_start(out_g[bass.ds(g, 1), b].rearrange("g n d -> (g n) d"),
                                 x_out[:, b]).then_inc(out_stored, 16)

            def iteration(i, load=True, store=True, after=True):
                if load:
                    sp.wait_ge(x_loaded, 16 * i + 32)
                    sp.wait_ge(drained, first_use(i) + (G_USES + GB if store else 0))
                    load_x(i + 2)
                if store:
                    store_out(i - 1, first_use(i) + PER - GB * (1 if after else 2))

            w_rows = w_lang.rearrange("(c p) n -> p c n", p=P)
            for c in range(C):
                sp.dma_start(raw_l[:, c], w_rows[:, c]).then_inc(w_loaded[f"l{c}"], 16)
            sp.dma_start(raw_g, w_grav.rearrange("(c p) n -> p c n", p=P)).then_inc(w_loaded["g"], 16)
            sp.dma_start(raw_o, w_o.rearrange("(c p) n -> p c n", p=P)).then_inc(w_loaded["o"], 16)
            load_x(0)
            sp.dma_start(raw_v, w_v.rearrange("(c p) n -> p c n", p=P)).then_inc(w_loaded["v"], 16)
            sp.wait_ge(x_loaded, 16)
            load_x(1)
            iteration(0, store=False)
            iteration(1)
            with sp.Fori(2, NG - 2) as i:
                iteration(i)
            iteration(NG - 2, load=False)
            iteration(NG - 1, load=False, after=False)
            store_out(NG - 1, first_use(NG))
            sp.wait_ge(out_stored, 16 * GB * NG)

        @block.gpsimd
        def _(pool):
            pool.memset(ident[:, :], 0.0).then_inc(ident_set, 1)
            pool.memset(diag_of[:, :, :], 0.0).then_inc(ident_set, 1)
            pool.memset(off_diag[:, :], 1.0).then_inc(ident_set, 1)
            pool.memset(neg_half[:, :], -0.5).then_inc(ident_set, 1)
            pool.memset(quarter[:, :], 0.25).then_inc(ident_set, 1)
            pool.memset(rn[:, :, :], 1.0).then_inc(ident_set, 1)
            pool.wait_ge(ident_set, 6)
            for m, fill in ((ident[:, :], 1.0), (diag_of[:, 0], 2.0), (diag_of[:, 1], -1.0), (off_diag[:, :], 0.0)):
                pool.affine_select(out=m, in_=m, compare_op=ALU.not_equal, fill=fill,
                                   base=0, pattern=[[-1, P]], channel_multiplier=1).then_inc(ident_ready, 1)

            def std_factors(g, bn, bn_done, t, step, b0=0, b1=GB, before=0):
                pool.wait_ge(bn_done, GB * g + b1)
                pool.tensor_tensor(t[:, SUM, b0:b1], bn[:, b0:b1, 1], bn[:, b0:b1, 4], ALU.add).then_inc(step, 1)
                pool.tensor_tensor(t[:, DIFF, b0:b1], bn[:, b0:b1, 1], bn[:, b0:b1, 4], ALU.subtract).then_inc(step, 1)
                pool.tensor_tensor(t[:, SQ, b0:b1], bn[:, b0:b1, 2], bn[:, b0:b1, 5], ALU.add).then_inc(step, 1)
                pool.wait_ge(step, LN_STEPS * g + before + 3)
                pool.tensor_tensor(t[:, DIFF4, b0:b1], t[:, DIFF, b0:b1], quarter[:, b0:b1], ALU.mult).then_inc(step, 1)
                pool.tensor_scalar(t[:, VAR_IN, b0:b1], t[:, SQ, b0:b1], 1.0 / D, EPS_LN, ALU.mult, ALU.add).then_inc(step, 1)
                pool.tensor_scalar(t[:, NEG_MEAN, b0:b1], t[:, SUM, b0:b1], -0.5, None, ALU.mult).then_inc(step, 1)
                pool.wait_ge(step, LN_STEPS * g + before + 4)
                pool.tensor_tensor(t[:, VAR_BETWEEN, b0:b1], t[:, DIFF4, b0:b1], t[:, DIFF, b0:b1], ALU.mult).then_inc(step, 1)
                pool.wait_ge(step, LN_STEPS * g + before + 7)
                pool.tensor_tensor(t[:, VAR, b0:b1], t[:, VAR_BETWEEN, b0:b1], t[:, VAR_IN, b0:b1], ALU.add).then_inc(step, 1)
                pool.wait_ge(step, LN_STEPS * g + before + 8)
                pool.tensor_tensor(t[:, RSTD, b0:b1], t[:, VAR, b0:b1], neg_half[:, b0:b1], ALU.pow).then_inc(step, 1)
                pool.wait_ge(step, LN_STEPS * g + before + 9)
                pool.tensor_tensor(t[:, SHIFT, b0:b1], t[:, NEG_MEAN, b0:b1], t[:, RSTD, b0:b1], ALU.mult).then_inc(step, 1)

            def norm1(g):
                wait_for(pool, h_ready, GB * g)
                std_factors(g, bn1, bn1_done, ln1, ln1_step)

            def add_bias(g, b):
                if b == 0:
                    wait_for(pool, out_stored, 16 * GB * g)
                pool.wait_ge(bn2_done, GB * g + b + 1)
                pool.tensor_tensor(x_out[:, b], x2[:, b], bias_sb[:, :], ALU.add).then_inc(x2b_ready, 1)

            def norm2(g):
                std_factors(g, bn2, bn2_done, ln2, ln2_step)

            def h2_lo(g, b):
                pool.wait_ge(h2_hi, GB * g + b + 1)
                pool.tensor_tensor(h2[1][:, b], h2f[:, b], h2[0][:, b].bitcast(F32), ALU.subtract)\
                    .then_inc(h2_split, 1)

            def diagonal(g):
                pool.wait_ge(p_copied, 2 * g + 2)
                wait_for(pool, sq_ready, 2 * g)
                select = diag_of[:, :, :].rearrange("p l m -> p (l m)").unsqueeze(1).to_broadcast([P, GB, 2 * P])
                pool.tensor_tensor(diag.rearrange("p b l m -> p b (l m)"),
                                   P_sb.rearrange("p b l m -> p b (l m)"), select, ALU.mult).then_inc(diag_ready, 1)

            def row_norms(g):
                pool.wait_ge(sq_ready, 2 * g + 2)
                wait_for(pool, k_ready, g)
                pool.tensor_tensor(rn[:, :, 0], sqc[:, :], neg_half[:, :], ALU.pow).then_inc(rn_step, 1)
                pool.wait_ge(rn_step, RN_STEPS * g + 1)
                pool.tensor_tensor(wr[:, :, :], rn[:, :, :], w8[:, :, :], ALU.mult).then_inc(rn_step, 1)

            def iteration(i, before=True, after=True):
                if after:
                    norm1(i + 1)
                if before:
                    for b in range(GB // 2):
                        add_bias(i - 1, b)
                    norm2(i - 1)
                diagonal(i)
                if before:
                    for b in range(GB // 2, GB):
                        add_bias(i - 1, b)
                row_norms(i)
                if before:
                    for b in range(GB):
                        h2_lo(i - 1, b)

            norm1(0)
            pool.wait_ge(scalars, 9)
            pool.wait_ge(consts_loaded, 16 * 4)
            iteration(0, before=False)
            iteration(1)
            with pool.Fori(2, NG - 1) as i:
                iteration(i)
            iteration(NG - 1, after=False)
            for q in range(2):
                std_factors(NG - 1, bn2, bn2_done, ln2, ln2_step, q * GB // 2, (q + 1) * GB // 2, q * LN_STEPS)
            for b in range(GB):
                add_bias(NG - 1, b)

        @block.scalar
        def _(act):
            act.dma_start(gate, gate_logit.unsqueeze(0).to_broadcast([P, 1])).then_inc(consts_loaded, 16)
            act.dma_start(lsig, log_sigma.unsqueeze(0).to_broadcast([P, 1])).then_inc(consts_loaded, 16)
            act.dma_start(adj_sb[:, :], adj).then_inc(consts_loaded, 16)
            act.dma_start(bias_sb[:, :], bias.unsqueeze(0).to_broadcast([P, D])).then_inc(consts_loaded, 16)

            def apply_norm1(g, wait_free=True):
                act.wait_ge(ln1_step, LN_STEPS * (g + 1))
                if wait_free:
                    act.wait_ge(t_done, GB * g)
                for b in range(GB):
                    xb = x_ring[:, bass.ds(g % SLOTS, 1), b].rearrange("p s d -> p (s d)")
                    act.activation(h[:, b], xb, ACT.Relu, bias=ln1[:, SHIFT, b:b + 1],
                                   scale=ln1[:, RSTD, b:b + 1]).then_inc(h_ready, 1)

            def t_hi(g, b, n):
                act.wait_ge(t_done, GB * g + b + 1)
                act.activation(hT[0][:, :, b], bank(n).rearrange("p (c m) -> p c m", c=C), ACT.Copy)\
                   .then_inc(hi_ready, 1)

            def iteration(i, before=True, after=True):
                n = 0
                if before:
                    act.wait_ge(p_done, GB * i)
                for a in range(C):
                    for l in range(2):
                        act.wait_ge(g_done, G_USES * i + n + 1)
                        act.activation(y[0][:, a, :, l], bank(n).rearrange("p (b m) -> p b m", b=GB), ACT.Copy)\
                           .then_inc(hi_ready, 1)
                        n += 1
                        if before and n == 4:
                            w_g_K_g(i - 1)
                        if before and n == G_USES - 1:
                            kt_copy(i - 1)
                for c in range(C):
                    if not before:
                        act.wait_ge(setup_mm, SETUP + c + 1)
                        act.activation(MT[0][:, c], bank(n), ACT.Copy).then_inc(hi_ready, 1)
                    n += 1
                if after:
                    apply_norm1(i + 1)
                if before:
                    act.wait_ge(s_ready, i)
                    act.wait_ge(diag_ready, i)
                for half in range(2):
                    act.wait_ge(p_done, GB * i + 2 * half + 2)
                    act.activation(P_sb[:, 2 * half:2 * half + 2], p_ps[:, 2 * half:2 * half + 2], ACT.Copy)\
                       .then_inc(p_copied, 1)
                if before:
                    h2_full(i - 1, 0)
                    h2_full(i - 1, 1)
                    act.wait_ge(kv_done, GB * i)
                for b in range(GB):
                    if not after and b == GB - 1:
                        exponentials(i)
                    act.wait_ge(v_done, GB * i + b + 1)
                    act.activation(v[0][:, b], bank(n), ACT.Copy).then_inc(hi_ready, 1)
                    n += 1
                    if after:
                        t_hi(i + 1, b, n)
                        n += 1
                    if before and b < 3:
                        for q in range(2 * b, 2 * b + 2):
                            (h2_full if b == 0 else h2_copy)(i - 1, q + 2 if b == 0 else q - 2)
                    if b == 0:
                        shift(i)
                if after:
                    exponentials(i)

            def h2_full(g, b, last=False):
                if b == 0 or last and b == GB // 2:
                    act.wait_ge(ln2_step, LN_STEPS * (g + 1 + b // (GB // 2)))
                if b == 0:
                    wait_for(act, h2_split, GB * g)
                act.activation(h2f[:, b], x2[:, b], ACT.Relu, bias=ln2[:, SHIFT, b:b + 1],
                               scale=ln2[:, RSTD, b:b + 1]).then_inc(h2_done, 1)

            def h2_copy(g, b):
                act.wait_ge(h2_done, GB * g + b + 1)
                if b == 0:
                    wait_for(act, l1_done, GB * g)
                act.activation(h2[0][:, b], h2f[:, b], ACT.Copy).then_inc(h2_hi, 1)

            def shift(g):
                act.wait_ge(sq_ready, 2 * g + 1)
                for b in range(GB):
                    e = act.activation(P_sb[:, b, 1], P_sb[:, b, 1], ACT.Identity, bias=sq[:, b, 1:2])
                e.then_inc(p_shifted, 1)

            def exponentials(g):
                act.wait_ge(s_ready, g + 1)
                act.activation(A[:, :, 1], A[:, :, 1], ACT.Exp, scale=inv_sig2).then_inc(exp_done, 1)

            def w_g_K_g(g):
                act.wait_ge(deg_step, 5 * g + 5)
                wait_for(act, kt_done, g)
                for b in range(GB):
                    e = act.activation(K[:, b], A[:, b, 1], ACT.Copy, scale=deg[:, 3, b, 1:2])
                e.then_inc(tg_ready, 1)

            def kt_copy(g):
                act.wait_ge(kt_done, g + 1)
                wait_for(act, kv_done, GB * g)
                act.activation(KT[0][:, :, :], kt_ps[:, :, :], ACT.Copy).then_inc(kt_hi, 1)

            def weight_hi(parts, raw, c, loaded):
                act.wait_ge(loaded, 16)
                act.activation(parts[0][:, c], raw[:, c], ACT.Copy).then_inc(w_hi, 1)

            def lw_hi(l, use):
                for c in range(C):
                    act.wait_ge(setup_mm, use + c + 1)
                    for a in range(c, C):
                        e = act.activation(Lw[0][:, l, blk[a, c]], bank(use + c)[:, (a - c) * P:(a - c + 1) * P],
                                           ACT.Copy, scale=0.5 if a == c else 1.0)
                    e.then_inc(hi_ready, 1)

            for c in range(C):
                weight_hi(wl_parts, raw_l, c, w_loaded[f"l{c}"])
            for c in range(C):
                weight_hi(wg_parts, raw_g, c, w_loaded["g"])
            lw_hi(0, 0)
            act.wait_ge(consts_loaded, 16 * 4)
            act.activation(egate, gate, ACT.Exp, scale=-1.0).then_inc(exp_gate, 1)
            act.activation(sig, lsig, ACT.Exp).then_inc(exp_gate, 1)
            for c in range(C):
                weight_hi(wv_parts, raw_v, c, w_loaded["v"])
            apply_norm1(0, wait_free=False)
            lw_hi(1, C)
            for c in range(C):
                act.wait_ge(setup_mm, 2 * C + c + 1)
                act.activation(woT_parts[0][:, c], bank(2 * C + c), ACT.Copy).then_inc(hi_ready, 1)
            for b in range(GB):
                t_hi(0, b, SETUP + b)
            act.wait_ge(a2_step, 1)
            act.activation(A2[0][:, :], adj2[:, :], ACT.Copy).then_inc(a2_hi, 1)

            iteration(0, before=False)
            iteration(1)
            with act.Fori(2, NG - 1) as i:
                iteration(i)
            iteration(NG - 1, after=False)
            w_g_K_g(NG - 1)
            kt_copy(NG - 1)
            for b in range(GB):
                h2_full(NG - 1, b, last=True)
                h2_copy(NG - 1, b)

        @block.vector
        def _(dve):
            def part(t):
                return t.bitcast(F32)

            def lo(out, ps, hi, n_hi, scale=None):
                dve.wait_ge(hi_ready, n_hi)
                if scale is None:
                    return dve.tensor_tensor(out, ps, part(hi), ALU.subtract)
                return dve.scalar_tensor_tensor(out=out, in0=ps, scalar=scale, in1=part(hi),
                                                op0=ALU.mult, op1=ALU.subtract)

            def t_lo(b, n, n_hi):
                return lo(hT[1][:, :, b], bank(n).rearrange("p (c m) -> p c m", c=C), hT[0][:, :, b], n_hi)

            def x_stats(g):
                dve.wait_ge(x_loaded, 16 * g + 16)
                wait_for(dve, ln1_step, LN_STEPS * g)
                for b in range(GB):
                    xb = x_ring[:, bass.ds(g % SLOTS, 1), b].rearrange("p s d -> p (s d)")
                    dve.bn_stats(bn1[:, b], xb).then_inc(bn1_done, 1)

            def similarities(g):
                dve.wait_ge(r_done, g + 1)
                dve.wait_ge(s_ready, g + 1)
                dve.tensor_tensor(A[:, :, 0], A[:, :, 0], r_ps[:, :, :], ALU.mult).then_inc(a_ready, 1)

            maskb = mask[:, :].unsqueeze(1).to_broadcast([P, GB, P])

            def mask_l(g):
                dve.wait_ge(a_ready, 3 * g + 1)
                dve.scalar_tensor_tensor(out=A[:, :, 0], in0=A[:, :, 0], scalar=0.0, in1=maskb,
                                         op0=ALU.max, op1=ALU.mult).then_inc(a_ready, 1)

            def mask_g(g):
                dve.wait_ge(exp_done, g + 1)
                dve.scalar_tensor_tensor(out=A[:, :, 1], in0=A[:, :, 1], scalar=1.0, in1=maskb,
                                         op0=ALU.min, op1=ALU.mult).then_inc(a_ready, 1)

            def row_factors(g):
                dve.wait_ge(a_ready, 3 * g + 3)
                dve.tensor_reduce(deg[:, 0], A, AX.X, ALU.add).then_inc(deg_step, 1)
                dve.wait_ge(deg_step, 5 * g + 1)
                dve.tensor_tensor(deg[:, 1], deg[:, 0], rn[:, :, :], ALU.mult).then_inc(deg_step, 1)
                dve.wait_ge(deg_step, 5 * g + 2)
                dve.tensor_scalar(deg[:, 1], deg[:, 1], EPS, None, ALU.max).then_inc(deg_step, 1)
                dve.wait_ge(deg_step, 5 * g + 3)
                dve.reciprocal(deg[:, 2], deg[:, 1]).then_inc(deg_step, 1)
                dve.wait_ge(deg_step, 5 * g + 4)
                dve.tensor_tensor(deg[:, 3], deg[:, 2], wr[:, :, :], ALU.mult).then_inc(deg_step, 1)

            def combine(g):
                dve.wait_ge(tg_ready, g + 1)
                for b in range(GB):
                    e = dve.scalar_tensor_tensor(out=K[:, b], in0=A[:, b, 0], scalar=deg[:, 3, b, 0:1],
                                                 in1=K[:, b], op0=ALU.mult, op1=ALU.add)
                e.then_inc(k_ready, 1)

            def kt_lo(g):
                dve.wait_ge(kt_hi, g + 1)
                dve.tensor_tensor(KT[1][:, :, :], kt_ps[:, :, :], part(KT[0][:, :, :]), ALU.subtract).then_inc(kt_split, 1)

            def residual(g, n, use, last=False):
                wait_for(dve, h2_done, GB * g)
                wait_for(dve, x2b_ready, GB * g)

                def add(b):
                    xb = x_ring[:, bass.ds(g % SLOTS, 1), b].rearrange("p s d -> p (s d)")
                    dve.wait_ge(kv_done, GB * g + b + 1)
                    dve.tensor_tensor(x2[:, b], bank(n + b), xb, ALU.add).then_inc(drained, 1)

                def stats(b):
                    dve.wait_ge(drained, use + b + 1)
                    dve.bn_stats(bn2[:, b], x2[:, b]).then_inc(bn2_done, 1)

                if last:
                    for b in range(GB):
                        add(b)
                        stats(b)
                    return
                add(0)
                for b in range(1, GB):
                    add(b)
                    stats(b - 1)
                stats(GB - 1)

            def h2_lo(g, b):
                dve.wait_ge(h2_hi, GB * g + b + 1)
                dve.tensor_tensor(h2[1][:, b], h2f[:, b], part(h2[0][:, b]), ALU.subtract).then_inc(h2_split, 1)

            def output(g, b, n):
                dve.wait_ge(l1_done, GB * g + b + 1)
                dve.wait_ge(x2b_ready, GB * g + b + 1)
                dve.tensor_tensor(x_out[:, b], bank(n), x_out[:, b], ALU.add).then_inc(drained, 1)

            def iteration(i, before=True, after=True):
                n = 0
                hi = first_hi(i)
                for a in range(C):
                    for l in range(2):
                        hi = hi + 1
                        lo(y[1][:, a, :, l], bank(n).rearrange("p (b m) -> p b m", b=GB), y[0][:, a, :, l], hi)\
                            .then_inc(drained, 1)
                        n += 1
                        if before and n == 1:
                            mask_g(i - 1)
                        if before and n == 2:
                            row_factors(i - 1)
                        if before and n == 4:
                            combine(i - 1)
                        if after and n == 6:
                            x_stats(i + 1)
                        if before and n == G_USES - 1:
                            kt_lo(i - 1)
                if before:
                    residual(i - 1, n, first_use(i) + n)
                else:
                    for c in range(C):
                        hi += 1
                        lo(MT[1][:, c], bank(n + c), MT[0][:, c], hi).then_inc(drained, 1)
                n += GB
                for b in range(GB):
                    hi = hi + 1
                    lo(v[1][:, b], bank(n), v[0][:, b], hi).then_inc(drained, 1)
                    n += 1
                    if after:
                        hi = hi + 1
                        t_lo(b, n, hi).then_inc(drained, 1 if before or b < GB - 1 else 1 + GB)
                        n += 1
                    if b == 0:
                        dve.wait_ge(diag_ready, i + 1)
                        wait_for(dve, rn_step, RN_STEPS * i)
                        wait_for(dve, p_shifted, i)
                        dve.tensor_reduce(sq[:, :, :], diag, AX.X, ALU.add).then_inc(sq_ready, 1)
                        dve.wait_ge(sq_ready, 2 * i + 1)
                        dve.tensor_scalar(sqc[:, :], sq[:, :, 0], EPS * EPS, None, ALU.max).then_inc(sq_ready, 1)
                    if b == (2 if after else 1):
                        dve.wait_ge(pt_done, i + 1)
                        dve.tensor_tensor(A, p_ps[:, :, :, :], P_sb, ALU.add).then_inc(s_ready, 1)
                    if not after and b == GB - 2:
                        similarities(i)
                        mask_l(i)
                if not after:
                    mask_g(i)
                    row_factors(i)
                    for b in range(GB):
                        output(i - 1, b, n + b)
                        if b == 1:
                            combine(i)
                    return
                if before:
                    output(i - 1, 0, n)
                    n += 1
                if before:
                    output(i - 1, 1, n)
                    output(i - 1, 2, n + 1)
                similarities(i)
                if before:
                    output(i - 1, 3, n + 2)
                mask_l(i)

            def weight_lo(parts, raw, c, n):
                dve.wait_ge(w_hi, n)
                dve.tensor_tensor(parts[1][:, c], raw[:, c], part(parts[0][:, c]), ALU.subtract).then_inc(w_split, 1)

            def lw_lo(l, use):
                for c in range(C):
                    for a in range(c, C):
                        e = lo(Lw[1][:, l, blk[a, c]], bank(use + c)[:, (a - c) * P:(a - c + 1) * P],
                               Lw[0][:, l, blk[a, c]], use + c + 1, 0.5 if a == c else 1.0)
                    e.then_inc(drained, 1)

            for c in range(C):
                weight_lo(wl_parts, raw_l, c, c + 1)
            for c in range(C):
                weight_lo(wg_parts, raw_g, c, C + c + 1)
            lw_lo(0, 0)
            x_stats(0)
            dve.wait_ge(ident_ready, 4)
            dve.wait_ge(consts_loaded, 16 * 4)
            dve.tensor_tensor(mask[:, :], adj_sb[:, :], off_diag[:, :], ALU.mult)
            dve.tensor_tensor(adj2[:, :], adj_sb[:, :], adj_sb[:, :], ALU.mult).then_inc(a2_step, 1)
            dve.wait_ge(exp_gate, 2)
            dve.tensor_scalar(w_l, egate, 1.0, None, ALU.add).then_inc(scalars, 1)
            dve.tensor_tensor(sig2, sig, sig, ALU.mult).then_inc(scalars, 1)
            dve.wait_ge(scalars, 2)
            dve.reciprocal(w_l, w_l).then_inc(scalars, 1)
            dve.reciprocal(inv_sig2, sig2).then_inc(scalars, 1)
            dve.wait_ge(scalars, 4)
            dve.tensor_scalar(w_g, w_l, -1.0, 1.0, ALU.mult, ALU.add).then_inc(scalars, 1)
            dve.wait_ge(scalars, 5)
            for b in range(GB):
                dve.tensor_copy(w8[:, b], scal[:, 2:4]).then_inc(scalars, 1)
            for c in range(C):
                weight_lo(wv_parts, raw_v, c, 2 * C + c + 1)
            lw_lo(1, C)
            for c in range(C):
                lo(woT_parts[1][:, c], bank(2 * C + c), woT_parts[0][:, c], 2 * C + c + 1).then_inc(drained, 1)
            for b in range(GB):
                t_lo(b, SETUP + b, SETUP + b + 1).then_inc(drained, 1)
            dve.wait_ge(a2_hi, 1)
            dve.tensor_tensor(A2[1][:, :], adj2[:, :], part(A2[0][:, :]), ALU.subtract).then_inc(a2_step, 1)

            iteration(0, before=False)
            iteration(1)
            with dve.Fori(2, NG - 1) as i:
                iteration(i)
            iteration(NG - 1, after=False)
            g = NG - 1
            kt_lo(g)
            use = first_use(g) + PER - GB
            residual(g, 0, use, last=True)
            for b in range(GB):
                h2_lo(g, b)
            for b in range(GB):
                output(g, b, b)

        @block.tensor
        def _(pe):
            def free(use):
                wait_for(pe, drained, use - BANKS + 1)

            def transposes_h(g, b, n, use):
                pe.wait_ge(h_ready, GB * g + b + 1)
                free(use)
                for c in range(C):
                    mm = pe.transpose(bank(n)[:, c * P:(c + 1) * P], h[:, b, c * P:(c + 1) * P], ident[:, :])
                mm.then_inc(t_done, 1)

            def product(out, terms):
                for k, (lhsT, rhs) in enumerate(terms):
                    mm = pe.matmul(out, lhsT, rhs, start=(k == 0), stop=(k == len(terms) - 1))
                return mm

            def y_block(a, l, n, use):
                free(use)
                product(bank(n), [t for c in range(a + 1) for t in passes(
                    [w[:, l, blk[a, c]] for w in Lw],
                    [w[:, c].rearrange("p b m -> p (b m)") for w in hT])]).then_inc(g_done, 1)

            def transposes_K(g):
                pe.wait_ge(k_ready, g + 1)
                for b in range(GB):
                    mm = pe.transpose(kt_ps[:, b], K[:, b], ident[:, :])
                mm.then_inc(kt_done, 1)

            def k_v(g, b, n, use):
                free(use)
                product(bank(n), passes([w[:, b] for w in KT], [w[:, b] for w in v])).then_inc(kv_done, 1)

            def layer1(g, b, n, use):
                pe.wait_ge(h2_split, GB * g + b + 1)
                free(use)
                product(bank(n), passes([w[:, :] for w in A2], [w[:, b] for w in h2])).then_inc(l1_done, 1)

            def transposes_rn(g):
                pe.wait_ge(rn_step, RN_STEPS * (g + 1))
                for b in range(GB):
                    mm = pe.transpose(r_ps[:, b], rn[:, b, 0:1].to_broadcast([P, P]), ident[:, :])
                mm.then_inc(r_done, 1)

            def iteration(i, before=True, after=True):
                n, use = 0, first_use(i)
                for a in range(C):
                    for l in range(2):
                        y_block(a, l, n, use + n)
                        n += 1
                        if before and n == G_USES - 1:
                            transposes_K(i - 1)
                if before:
                    pe.wait_ge(kt_split, i)
                    for b in range(GB):
                        k_v(i - 1, b, n + b, use + n + b)
                else:
                    for c in range(C):
                        free(use + n + c)
                        product(bank(n + c), [t for e in range(C) for t in passes(
                            [w[:, e, c * P:(c + 1) * P] for w in wv_parts], [w[:, e] for w in woT_parts])])\
                            .then_inc(setup_mm, 1)
                n += GB
                pe.wait_ge(drained, use + G_USES)
                for b in range(GB):
                    product(p_ps[:, b].rearrange("p l m -> p (l m)"), [t for a in range(C) for t in passes(
                        [w[:, a, b] for w in hT],
                        [w[:, a, b].rearrange("p l m -> p (l m)") for w in y])]).then_inc(p_done, 1)
                if not before:
                    pe.wait_ge(drained, use + G_USES + C)
                for b in range(GB):
                    free(use + n)
                    product(bank(n), [t for c in range(C) for t in passes(
                        [w[:, c, b] for w in hT], [w[:, c] for w in MT])]).then_inc(v_done, 1)
                    n += 1
                    if not after and b == GB - 2:
                        transposes_rn(i)
                    if b == (2 if after else 1):
                        pe.wait_ge(p_shifted, i + 1)
                        for k in range(2 * GB):
                            mm = pe.transpose(p_ps[:, k // 2, k % 2], P_sb[:, k // 2, k % 2], ident[:, :])
                        mm.then_inc(pt_done, 1)
                    if after:
                        transposes_h(i + 1, b, n, use + n)
                        n += 1
                if after:
                    transposes_rn(i)
                if before:
                    for b in range(GB):
                        layer1(i - 1, b, n + b, use + n + b)

            for l, parts in enumerate((wl_parts, wg_parts)):
                for e in range(C):
                    pe.wait_ge(w_split, C * l + e + 1)
                    for c in range(C):
                        if e == 0:
                            free(C * l + c)
                        for k, (lhsT, rhs) in enumerate(passes([w[:, e, c * P:(c + 1) * P] for w in parts],
                                                               [w[:, e, c * P:D] for w in parts])):
                            mm = pe.matmul(bank(C * l + c)[:, 0:D - c * P], lhsT, rhs,
                                           start=(e == 0 and k == 0), stop=(e == C - 1 and k == 2))
                        if e == C - 1:
                            mm.then_inc(setup_mm, 1)
            pe.wait_ge(w_loaded["o"], 16)
            pe.wait_ge(ident_ready, 4)
            for c in range(C):
                free(2 * C + c)
                for q in range(C):
                    mm = pe.transpose(bank(2 * C + c)[:, q * P:(q + 1) * P], raw_o[:, q, c * P:(c + 1) * P], ident[:, :])
                mm.then_inc(setup_mm, 1)
            for b in range(GB):
                transposes_h(0, b, SETUP + b, SETUP + b)
            pe.wait_ge(drained, SETUP + GB)

            iteration(0, before=False)
            pe.wait_ge(a2_step, 2)
            iteration(1)
            with pe.Fori(2, NG - 1) as i:
                iteration(i)
            iteration(NG - 1, after=False)
            g = NG - 1
            use = first_use(g) + PER - GB
            transposes_K(g)
            pe.wait_ge(kt_split, NG)
            for b in range(GB):
                k_v(g, b, b, use + b)
            for b in range(GB):
                layer1(g, b, b, use + GB + b)


_INS = ["x", "adj", "L0_gnn_W_lang", "L0_gnn_W_grav", "L0_gnn_W_V", "L0_gnn_W_O",
        "L0_gnn_gate_logit", "L0_gnn_log_sigma", "L1_gnn_bias"]


def kernel(**inputs):
    import numpy as np
    import concourse.bacc as bacc
    from concourse.bass_utils import run_bass_kernel_spmd

    nc = bacc.Bacc("TRN2", target_bir_lowering=False, num_devices=1)
    arrays, args = {}, []
    for name in _INS:
        a = np.ascontiguousarray(inputs[name])
        if a.ndim == 0:
            a = a.reshape(1)
        arrays[f"in_{name}"] = a
        args.append(nc.dram_tensor(f"in_{name}", a.shape, mybir.dt.from_np(a.dtype), kind="ExternalInput").ap())
    out = nc.dram_tensor("out", arrays["in_x"].shape, F32, kind="ExternalOutput").ap()
    gnn_pair(nc, *args, out)
    r = run_bass_kernel_spmd(nc, [arrays], core_ids=[0])
    return r.results[0]["out"]
```

```python
from contextlib import ExitStack

import concourse.bass as bass
from concourse import mybir

ALU = mybir.AluOpType
ACT = mybir.ActivationFunctionType
AX = mybir.AxisListType
F32 = mybir.dt.float32
F32R = mybir.dt.float32r

P = 128
GB = 4
SLOTS = 3
BANKS = 4
EPS_LN = 1e-5
EPS = 1e-8


def gnn_pair(nc, x, adj, w_lang, w_grav, w_v, w_o, gate_logit, log_sigma, bias, out):
    B, N, D = x.shape
    assert N == P and B % GB == 0 and D % P == 0 and D <= 512 and D // P == GB
    C = D // P
    NG = B // GB
    TRI = [(a, c) for a in range(C) for c in range(a + 1)]
    SUM, DIFF, SQ, DIFF4, VAR_IN, NEG_MEAN, VAR_BETWEEN, VAR, RSTD, SHIFT = range(10)
    LN_STEPS = 10
    LAST_STEPS = 7
    RN_STEPS = 2
    blk = {ac: n for n, ac in enumerate(TRI)}

    G_USES = 2 * C
    SETUP = C
    PER = G_USES + GB + 2 * GB + GB

    def first_use(i):
        return SETUP + GB + PER * i

    HI_PER = G_USES + 2 * GB

    def first_hi(i):
        return SETUP + GB + HI_PER * i + (C if not isinstance(i, int) or i else 0)

    x_g = x.rearrange("(g b) n d -> g n b d", b=GB)
    out_g = out.rearrange("(g b) n d -> g b n d", b=GB)

    with ExitStack() as ctx:
        def sb(name, shape, dt=F32):
            return ctx.enter_context(nc.sbuf_tensor(name, shape, dt))

        def sem(name):
            return ctx.enter_context(nc.semaphore(name))

        x_ring = sb("x_ring", [P, SLOTS, GB, D])
        h = sb("h", [P, GB, D])
        hT = [sb(f"hT_{s}", [P, C, GB, P], F32R) for s in ("hi", "lo")]
        y = [sb(f"y_{s}", [P, C, GB, 2, P], F32R) for s in ("hi", "lo")]
        Lw = [sb(f"Lw_{s}", [P, 2, len(TRI), P], F32R) for s in ("hi", "lo")]
        MT = [sb(f"MT_{s}", [P, C, D], F32R) for s in ("hi", "lo")]
        v = [sb(f"v_{s}", [P, GB, D], F32R) for s in ("hi", "lo")]
        chain = sb("chain", [P, 3, GB, 2, P])
        P_sb, diag, A = (chain[:, n] for n in range(3))
        K = sb("K", [P, GB, P])
        KT = [sb(f"KT_{s}", [P, GB, P], F32R) for s in ("hi", "lo")]
        x2 = sb("x2", [P, GB, D])
        x_out = sb("x_out", [P, GB, D])
        h2f = sb("h2f", [P, GB, D])
        h2 = [sb(f"h2_{s}", [P, GB, D], F32R) for s in ("hi", "lo")]
        adj_sb = sb("adj_sb", [P, P])
        ident = sb("ident", [P, P])
        diag_of = sb("diag_of", [P, 2, P])
        off_diag = sb("off_diag", [P, P])
        mask = sb("mask", [P, P])
        adj2 = sb("adj2", [P, P])
        A2 = [sb(f"A2_{s}", [P, P], F32R) for s in ("hi", "lo")]
        bias_sb = sb("bias_sb", [P, D])
        scal = sb("scal", [P, 8])
        gate, lsig, w_l, w_g, egate, sig, sig2, inv_sig2 = (scal[:, n:n + 1] for n in range(8))
        w8 = sb("w8", [P, GB, 2])
        bn1 = sb("bn1", [P, GB, 6])
        bn2 = sb("bn2", [P, GB, 6])
        ln1 = sb("ln1", [P, LN_STEPS, GB])
        ln2 = sb("ln2", [P, LN_STEPS, GB])
        neg_half = sb("neg_half", [P, GB])
        quarter = sb("quarter", [P, GB])
        sq = sb("sq", [P, GB, 2])
        sqc = sb("sqc", [P, GB])
        rn = sb("rn", [P, GB, 2])
        wr = sb("wr", [P, GB, 2])
        deg = sb("deg", [P, 4, GB, 2])

        raw_l = x2[:, :, :]
        raw_g = h2f[:, :, :]
        raw_v = x_ring[:, SLOTS - 1]
        raw_o = chain[:, 0:2].rearrange("p a b l m -> p (a b l m)").rearrange("p (c n) -> p c n", c=C)
        y_rows = [w[:, :, :, :, :].rearrange("p c b l m -> p (c b l m)").rearrange("p (q n) -> p q n", n=D)
                  for w in y]
        wl_parts = [w[:, 0:C] for w in y_rows]
        wg_parts = [w[:, C:2 * C] for w in y_rows]
        wv_parts = [w[:, :, :] for w in v]
        woT_parts = [w[:, :, :] for w in h2]

        ring = ctx.enter_context(nc.psum_tensor("ring", [P, BANKS, 512], F32))
        p_ps = ctx.enter_context(nc.psum_tensor("p_ps", [P, GB, 2, P], F32))
        r_ps = ctx.enter_context(nc.psum_tensor("r_ps", [P, GB, P], F32))
        kt_ps = ctx.enter_context(nc.psum_tensor("kt_ps", [P, GB, P], F32))

        def bank(use):
            return ring[:, use % BANKS]

        side = [p_ps[:, 0:2].rearrange("p b l m -> p (b l m)"), p_ps[:, 2:4].rearrange("p b l m -> p (b l m)"),
                r_ps[:, :, :].rearrange("p b m -> p (b m)"), kt_ps[:, :, :].rearrange("p b m -> p (b m)")]

        x_loaded, consts_loaded = sem("x_loaded"), sem("consts_loaded")
        w_loaded = {s: sem(f"w_loaded_{s}") for s in ("l0", "l1", "l2", "l3", "g", "o", "v")}
        side_hi, side_split = sem("side_hi"), sem("side_split")
        w_hi, w_split = sem("w_hi"), sem("w_split")
        out_stored = sem("out_stored")
        ident_set, ident_ready = sem("ident_set"), sem("ident_ready")
        exp_gate, scalars, a2_step, a2_hi = sem("exp_gate"), sem("scalars"), sem("a2_step"), sem("a2_hi")
        drained = sem("drained")
        hi_ready = sem("hi_ready")
        setup_mm = sem("setup_mm")
        t_done, g_done, p_done, v_done = sem("t_done"), sem("g_done"), sem("p_done"), sem("v_done")
        pt_done, r_done, kt_done, kv_done, l1_done = (
            sem("pt_done"), sem("r_done"), sem("kt_done"), sem("kv_done"), sem("l1_done"))
        h_ready = sem("h_ready")
        p_copied = sem("p_copied")
        exp_done = sem("exp_done")
        tg_ready = sem("tg_ready")
        kt_hi = sem("kt_hi")
        h2_hi = sem("h2_hi")
        bn1_done, bn2_done = sem("bn1_done"), sem("bn2_done")
        p_shifted = sem("p_shifted")
        s_ready = sem("s_ready")
        sq_ready = sem("sq_ready")
        a_ready = sem("a_ready")
        deg_step = sem("deg_step")
        k_ready = sem("k_ready")
        kt_split = sem("kt_split")
        h2_split = sem("h2_split")
        ln1_step, ln2_step = sem("ln1_step"), sem("ln2_step")
        h2_split_dve = sem("h2_split_dve")
        ln2_last = sem("ln2_last")
        ln2_rstd = sem("ln2_rstd")
        h2_done = sem("h2_done")
        x2b_ready = sem("x2b_ready")
        diag_ready = sem("diag_ready")
        rn_step = sem("rn_step")

        def passes(hi_lo_lhs, hi_lo_rhs):
            return [(hi_lo_lhs[0], hi_lo_rhs[0]), (hi_lo_lhs[0], hi_lo_rhs[1]), (hi_lo_lhs[1], hi_lo_rhs[0])]

        def wait_for(eng, sem, count):
            if not isinstance(count, int) or count > 0:
                eng.wait_ge(sem, count)

        block = ctx.enter_context(nc.Block())

        @block.sync
        def _(sp):
            def load_x(g):
                sp.dma_start(x_ring[:, bass.ds(g % SLOTS, 1)].rearrange("p s b d -> p (s b) d"),
                             x_g[bass.ds(g, 1)].rearrange("g n b d -> (g n) b d")).then_inc(x_loaded, 16)

            def store_out(g, use):
                for b in range(GB):
                    sp.wait_ge(drained, use + b + 1)
                    sp.dma_start(out_g[bass.ds(g, 1), b].rearrange("g n d -> (g n) d"),
                                 x_out[:, b]).then_inc(out_stored, 16)

            def iteration(i, load=True, store=True, after=True):
                if load:
                    sp.wait_ge(x_loaded, 16 * i + 32)
                    if store:
                        sp.wait_ge(drained, first_use(i) + G_USES + GB)
                    else:
                        sp.wait_ge(w_split, 3 * C)
                    load_x(i + 2)
                if store:
                    store_out(i - 1, first_use(i) + PER - GB * (1 if after else 2))

            w_rows = w_lang.rearrange("(c p) n -> p c n", p=P)
            for c in range(C):
                sp.dma_start(raw_l[:, c], w_rows[:, c]).then_inc(w_loaded[f"l{c}"], 16)
            sp.dma_start(raw_g, w_grav.rearrange("(c p) n -> p c n", p=P)).then_inc(w_loaded["g"], 16)
            load_x(0)
            sp.dma_start(raw_o, w_o.rearrange("(c p) n -> p c n", p=P)).then_inc(w_loaded["o"], 16)
            sp.dma_start(raw_v, w_v.rearrange("(c p) n -> p c n", p=P)).then_inc(w_loaded["v"], 16)
            sp.wait_ge(x_loaded, 16)
            load_x(1)
            iteration(0, store=False)
            iteration(1)
            with sp.Fori(2, NG - 2) as i:
                iteration(i)
            iteration(NG - 2, load=False)
            iteration(NG - 1, load=False, after=False)
            store_out(NG - 1, first_use(NG))
            sp.wait_ge(out_stored, 16 * GB * NG)

        @block.gpsimd
        def _(pool):
            pool.memset(ident[:, :], 0.0).then_inc(ident_set, 1)
            pool.memset(diag_of[:, :, :], 0.0).then_inc(ident_set, 1)
            pool.memset(off_diag[:, :], 1.0).then_inc(ident_set, 1)
            pool.memset(neg_half[:, :], -0.5).then_inc(ident_set, 1)
            pool.memset(quarter[:, :], 0.25).then_inc(ident_set, 1)
            pool.memset(rn[:, :, :], 1.0).then_inc(ident_set, 1)
            pool.wait_ge(ident_set, 6)
            for m, fill in ((ident[:, :], 1.0), (diag_of[:, 0], 2.0), (diag_of[:, 1], -1.0), (off_diag[:, :], 0.0)):
                pool.affine_select(out=m, in_=m, compare_op=ALU.not_equal, fill=fill,
                                   base=0, pattern=[[-1, P]], channel_multiplier=1).then_inc(ident_ready, 1)

            def std_factors(g, bn, bn_done, t, step):
                pool.wait_ge(bn_done, GB * (g + 1))
                pool.tensor_tensor(t[:, SUM], bn[:, :, 1], bn[:, :, 4], ALU.add).then_inc(step, 1)
                pool.tensor_tensor(t[:, DIFF], bn[:, :, 1], bn[:, :, 4], ALU.subtract).then_inc(step, 1)
                pool.tensor_tensor(t[:, SQ], bn[:, :, 2], bn[:, :, 5], ALU.add).then_inc(step, 1)
                pool.wait_ge(step, LN_STEPS * g + 3)
                pool.tensor_tensor(t[:, DIFF4], t[:, DIFF], quarter[:, :], ALU.mult).then_inc(step, 1)
                pool.tensor_scalar(t[:, VAR_IN], t[:, SQ], 1.0 / D, EPS_LN, ALU.mult, ALU.add).then_inc(step, 1)
                pool.tensor_scalar(t[:, NEG_MEAN], t[:, SUM], -0.5, None, ALU.mult).then_inc(step, 1)
                pool.wait_ge(step, LN_STEPS * g + 4)
                pool.tensor_tensor(t[:, VAR_BETWEEN], t[:, DIFF4], t[:, DIFF], ALU.mult).then_inc(step, 1)
                pool.wait_ge(step, LN_STEPS * g + 7)
                pool.tensor_tensor(t[:, VAR], t[:, VAR_BETWEEN], t[:, VAR_IN], ALU.add).then_inc(step, 1)
                pool.wait_ge(step, LN_STEPS * g + 8)
                pool.tensor_tensor(t[:, RSTD], t[:, VAR], neg_half[:, :], ALU.pow).then_inc(step, 1)
                pool.wait_ge(step, LN_STEPS * g + 9)
                pool.tensor_tensor(t[:, SHIFT], t[:, NEG_MEAN], t[:, RSTD], ALU.mult).then_inc(step, 1)

            def norm1(g):
                wait_for(pool, h_ready, GB * g)
                std_factors(g, bn1, bn1_done, ln1, ln1_step)

            def add_bias(g, b):
                if b == 0:
                    wait_for(pool, out_stored, 16 * GB * g)
                pool.wait_ge(bn2_done, GB * g + b + 1)
                pool.tensor_tensor(x_out[:, b], x2[:, b], bias_sb[:, :], ALU.add).then_inc(x2b_ready, 1)

            def norm2(g):
                std_factors(g, bn2, bn2_done, ln2, ln2_step)

            def h2_lo(g, b):
                pool.wait_ge(h2_hi, GB * g + b + 1)
                pool.tensor_tensor(h2[1][:, b], h2f[:, b], h2[0][:, b].bitcast(F32), ALU.subtract)\
                    .then_inc(h2_split, 1)

            def diagonal(g):
                pool.wait_ge(p_copied, 2 * g + 2)
                wait_for(pool, sq_ready, 2 * g)
                select = diag_of[:, :, :].rearrange("p l m -> p (l m)").unsqueeze(1).to_broadcast([P, GB, 2 * P])
                pool.tensor_tensor(diag.rearrange("p b l m -> p b (l m)"),
                                   P_sb.rearrange("p b l m -> p b (l m)"), select, ALU.mult).then_inc(diag_ready, 1)

            def row_norms(g, steps):
                pool.wait_ge(sq_ready, 2 * g + steps)
                wait_for(pool, k_ready, g)
                pool.tensor_tensor(rn[:, :, 0], sqc[:, :], neg_half[:, :], ALU.pow).then_inc(rn_step, 1)
                pool.wait_ge(rn_step, RN_STEPS * g + 1)
                pool.tensor_tensor(wr[:, :, :], rn[:, :, :], w8[:, :, :], ALU.mult).then_inc(rn_step, 1)

            def iteration(i, before=True, after=True):
                if after:
                    norm1(i + 1)
                if before:
                    for b in range(GB // 2):
                        add_bias(i - 1, b)
                    norm2(i - 1)
                if after:
                    diagonal(i)
                if not after:
                    row_norms(i, 3)
                if before:
                    for b in range(GB // 2, GB):
                        add_bias(i - 1, b)
                if after:
                    row_norms(i, 2)
                if before:
                    for b in range(GB):
                        h2_lo(i - 1, b)

            norm1(0)
            pool.wait_ge(scalars, 9)
            pool.wait_ge(consts_loaded, 16 * 4)
            iteration(0, before=False)
            iteration(1)
            with pool.Fori(2, NG - 1) as i:
                iteration(i)
            iteration(NG - 1, after=False)
            g = NG - 1

            def last_factors(q):
                b0, b1 = q * GB // 2, (q + 1) * GB // 2
                pool.wait_ge(ln2_last, LAST_STEPS * (q + 1))
                pool.tensor_tensor(ln2[:, RSTD, b0:b1], ln2[:, VAR, b0:b1], neg_half[:, b0:b1], ALU.pow)\
                    .then_inc(ln2_rstd, 1)
                pool.wait_ge(ln2_rstd, 2 * q + 1)
                pool.tensor_tensor(ln2[:, SHIFT, b0:b1], ln2[:, NEG_MEAN, b0:b1], ln2[:, RSTD, b0:b1], ALU.mult)\
                    .then_inc(ln2_rstd, 1)

            last_factors(0)
            for b in range(GB // 2):
                add_bias(g, b)
            last_factors(1)
            for b in range(GB // 2, GB):
                add_bias(g, b)

        @block.scalar
        def _(act):
            act.dma_start(gate, gate_logit.unsqueeze(0).to_broadcast([P, 1])).then_inc(consts_loaded, 16)
            act.dma_start(lsig, log_sigma.unsqueeze(0).to_broadcast([P, 1])).then_inc(consts_loaded, 16)
            act.dma_start(adj_sb[:, :], adj).then_inc(consts_loaded, 16)
            act.dma_start(bias_sb[:, :], bias.unsqueeze(0).to_broadcast([P, D])).then_inc(consts_loaded, 16)

            def apply_norm1(g, wait_free=True):
                act.wait_ge(ln1_step, LN_STEPS * (g + 1))
                if wait_free:
                    act.wait_ge(t_done, GB * g)
                for b in range(GB):
                    xb = x_ring[:, bass.ds(g % SLOTS, 1), b].rearrange("p s d -> p (s d)")
                    act.activation(h[:, b], xb, ACT.Relu, bias=ln1[:, SHIFT, b:b + 1],
                                   scale=ln1[:, RSTD, b:b + 1]).then_inc(h_ready, 1)

            def t_hi(g, b, n):
                act.wait_ge(t_done, GB * g + b + 1)
                act.activation(hT[0][:, :, b], bank(n).rearrange("p (c m) -> p c m", c=C), ACT.Copy)\
                   .then_inc(hi_ready, 1)

            def iteration(i, before=True, after=True):
                n = 0
                if before:
                    act.wait_ge(p_done, GB * i)
                for a in range(C):
                    for l in range(2):
                        act.wait_ge(g_done, G_USES * i + n + 1)
                        act.activation(y[0][:, a, :, l], bank(n).rearrange("p (b m) -> p b m", b=GB), ACT.Copy)\
                           .then_inc(hi_ready, 1)
                        n += 1
                        if not before and G_USES - C <= n < G_USES:
                            factor_hi(2 * (n - G_USES + C))
                            factor_hi(2 * (n - G_USES + C) + 1)
                        if before and n == 4:
                            w_g_K_g(i - 1)
                        if before and n == G_USES - 1:
                            kt_copy(i - 1)
                for c in range(C):
                    if not before:
                        act.wait_ge(setup_mm, 3 * C + c + 1)
                        act.activation(MT[0][:, c], bank(n), ACT.Copy).then_inc(hi_ready, 1)
                    n += 1
                if after:
                    apply_norm1(i + 1)
                if before:
                    act.wait_ge(s_ready, i)
                    act.wait_ge(diag_ready, i)
                for half in range(2):
                    act.wait_ge(p_done, GB * i + 2 * half + 2)
                    act.activation(P_sb[:, 2 * half:2 * half + 2], p_ps[:, 2 * half:2 * half + 2], ACT.Copy)\
                       .then_inc(p_copied, 1)
                if not after:
                    shift(i, 2)
                if before:
                    h2_full(i - 1, 0)
                    h2_full(i - 1, 1)
                    act.wait_ge(kv_done, GB * i)
                for b in range(GB):
                    if not after and b == 1:
                        exponentials(i)
                    act.wait_ge(v_done, GB * i + b + 1)
                    act.activation(v[0][:, b], bank(n), ACT.Copy).then_inc(hi_ready, 1)
                    n += 1
                    if after:
                        t_hi(i + 1, b, n)
                        n += 1
                    if not after and b == GB - 2:
                        w_g_K_g(i)
                    if before and b < 3:
                        for q in range(2 * b, 2 * b + 2):
                            (h2_full if b == 0 else h2_copy)(i - 1, q + 2 if b == 0 else q - 2)
                    if b == 0 and after:
                        shift(i, 1)
                if after:
                    exponentials(i)

            def h2_full(g, b, last=False):
                if last:
                    act.wait_ge(ln2_rstd, 2 * (1 + b // (GB // 2)))
                elif b == 0:
                    act.wait_ge(ln2_step, LN_STEPS * (g + 1))
                if b == 0:
                    wait_for(act, h2_split, GB * g)
                act.activation(h2f[:, b], x2[:, b], ACT.Relu, bias=ln2[:, SHIFT, b:b + 1],
                               scale=ln2[:, RSTD, b:b + 1]).then_inc(h2_done, 1)

            def h2_copy(g, b):
                act.wait_ge(h2_done, GB * g + b + 1)
                if b == 0:
                    wait_for(act, l1_done, GB * g)
                act.activation(h2[0][:, b], h2f[:, b], ACT.Copy).then_inc(h2_hi, 1)

            def shift(g, parts):
                act.wait_ge(sq_ready, 2 * g + parts)
                for b in range(GB):
                    e = act.activation(P_sb[:, b, 1], P_sb[:, b, 1], ACT.Identity, bias=sq[:, b, 1:2])
                e.then_inc(p_shifted, 1)

            def exponentials(g):
                act.wait_ge(s_ready, g + 1)
                act.activation(A[:, :, 1], A[:, :, 1], ACT.Exp, scale=inv_sig2).then_inc(exp_done, 1)

            def w_g_K_g(g):
                act.wait_ge(deg_step, 5 * g + 5)
                wait_for(act, kt_done, g)
                for b in range(GB):
                    e = act.activation(K[:, b], A[:, b, 1], ACT.Copy, scale=deg[:, 3, b, 1:2])
                e.then_inc(tg_ready, 1)

            def kt_copy(g):
                act.wait_ge(kt_done, g + 1)
                wait_for(act, kv_done, GB * g)
                act.activation(KT[0][:, :, :], kt_ps[:, :, :], ACT.Copy).then_inc(kt_hi, 1)

            def weight_hi(parts, raw, c, loaded):
                act.wait_ge(loaded, 16)
                act.activation(parts[0][:, c], raw[:, c], ACT.Copy).then_inc(w_hi, 1)

            def factor_hi(q):
                if q < C:
                    weight_hi(wv_parts, raw_v, q, w_loaded["v"])
                else:
                    act.wait_ge(setup_mm, 2 * C + q - C + 1)
                    act.activation(woT_parts[0][:, q - C], side[q - C], ACT.Copy).then_inc(side_hi, 1)

            def lw_hi(l, banks, done):
                for c in range(C):
                    act.wait_ge(setup_mm, C * l + c + 1)
                    for a in range(c, C):
                        e = act.activation(Lw[0][:, l, blk[a, c]], banks[c][:, (a - c) * P:(a - c + 1) * P],
                                           ACT.Copy, scale=0.5 if a == c else 1.0)
                    e.then_inc(done, 1)

            for c in range(C):
                weight_hi(wl_parts, raw_l, c, w_loaded[f"l{c}"])
            for c in range(C):
                weight_hi(wg_parts, raw_g, c, w_loaded["g"])
            lw_hi(0, [bank(c) for c in range(C)], hi_ready)
            act.wait_ge(consts_loaded, 16 * 4)
            act.activation(egate, gate, ACT.Exp, scale=-1.0).then_inc(exp_gate, 1)
            act.activation(sig, lsig, ACT.Exp).then_inc(exp_gate, 1)
            apply_norm1(0, wait_free=False)
            lw_hi(1, side, side_hi)
            for b in range(GB):
                t_hi(0, b, SETUP + b)
            act.wait_ge(a2_step, 1)
            act.activation(A2[0][:, :], adj2[:, :], ACT.Copy).then_inc(a2_hi, 1)

            iteration(0, before=False)
            iteration(1)
            with act.Fori(2, NG - 1) as i:
                iteration(i)
            iteration(NG - 1, after=False)
            kt_copy(NG - 1)
            for b in range(GB):
                h2_full(NG - 1, b, last=True)
                h2_copy(NG - 1, b)

        @block.vector
        def _(dve):
            def part(t):
                return t.bitcast(F32)

            def lo(out, ps, hi, n_hi):
                dve.wait_ge(hi_ready, n_hi)
                return dve.tensor_tensor(out, ps, part(hi), ALU.subtract)

            def t_lo(b, n, n_hi):
                return lo(hT[1][:, :, b], bank(n).rearrange("p (c m) -> p c m", c=C), hT[0][:, :, b], n_hi)

            def x_stats(g):
                dve.wait_ge(x_loaded, 16 * g + 16)
                wait_for(dve, ln1_step, LN_STEPS * g)
                for b in range(GB):
                    xb = x_ring[:, bass.ds(g % SLOTS, 1), b].rearrange("p s d -> p (s d)")
                    dve.bn_stats(bn1[:, b], xb).then_inc(bn1_done, 1)

            def similarities(g):
                dve.wait_ge(r_done, g + 1)
                dve.wait_ge(s_ready, g + 1)
                dve.tensor_tensor(A[:, :, 0], A[:, :, 0], r_ps[:, :, :], ALU.mult).then_inc(a_ready, 1)

            maskb = mask[:, :].unsqueeze(1).to_broadcast([P, GB, P])

            def mask_l(g):
                dve.wait_ge(a_ready, 3 * g + 1)
                dve.scalar_tensor_tensor(out=A[:, :, 0], in0=A[:, :, 0], scalar=0.0, in1=maskb,
                                         op0=ALU.max, op1=ALU.mult).then_inc(a_ready, 1)

            def mask_g(g):
                dve.wait_ge(exp_done, g + 1)
                dve.scalar_tensor_tensor(out=A[:, :, 1], in0=A[:, :, 1], scalar=1.0, in1=maskb,
                                         op0=ALU.min, op1=ALU.mult).then_inc(a_ready, 1)

            def row_factors(g):
                dve.wait_ge(a_ready, 3 * g + 3)
                dve.tensor_reduce(deg[:, 0], A, AX.X, ALU.add).then_inc(deg_step, 1)
                dve.wait_ge(deg_step, 5 * g + 1)
                dve.tensor_tensor(deg[:, 1], deg[:, 0], rn[:, :, :], ALU.mult).then_inc(deg_step, 1)
                dve.wait_ge(deg_step, 5 * g + 2)
                dve.tensor_scalar(deg[:, 1], deg[:, 1], EPS, None, ALU.max).then_inc(deg_step, 1)
                dve.wait_ge(deg_step, 5 * g + 3)
                dve.reciprocal(deg[:, 2], deg[:, 1]).then_inc(deg_step, 1)
                dve.wait_ge(deg_step, 5 * g + 4)
                dve.tensor_tensor(deg[:, 3], deg[:, 2], wr[:, :, :], ALU.mult).then_inc(deg_step, 1)

            def combine(g):
                dve.wait_ge(tg_ready, g + 1)
                for b in range(GB):
                    e = dve.scalar_tensor_tensor(out=K[:, b], in0=A[:, b, 0], scalar=deg[:, 3, b, 0:1],
                                                 in1=K[:, b], op0=ALU.mult, op1=ALU.add)
                e.then_inc(k_ready, 1)

            def kt_lo(g):
                dve.wait_ge(kt_hi, g + 1)
                dve.tensor_tensor(KT[1][:, :, :], kt_ps[:, :, :], part(KT[0][:, :, :]), ALU.subtract).then_inc(kt_split, 1)

            def residual(g, n, use, last=False):
                wait_for(dve, h2_done, GB * g)
                wait_for(dve, x2b_ready, GB * g)

                def add(b):
                    xb = x_ring[:, bass.ds(g % SLOTS, 1), b].rearrange("p s d -> p (s d)")
                    dve.wait_ge(kv_done, GB * g + b + 1)
                    dve.tensor_tensor(x2[:, b], bank(n + b), xb, ALU.add).then_inc(drained, 1)

                def stats(b):
                    dve.wait_ge(drained, use + b + 1)
                    dve.bn_stats(bn2[:, b], x2[:, b]).then_inc(bn2_done, 1)

                if last:
                    for b in range(GB):
                        add(b)
                        stats(b)
                        if b % 2 == 1:
                            last_factors(b - 1, b + 1, b // 2 * LAST_STEPS)
                    return
                add(0)
                for b in range(1, GB):
                    add(b)
                    stats(b - 1)
                stats(GB - 1)

            def last_factors(b0, b1, before):
                t = [ln2[:, n, b0:b1] for n in range(LN_STEPS)]
                m0, m1, q0, q1 = (bn2[:, b0:b1, n] for n in (1, 4, 2, 5))
                dve.wait_ge(ln2_step, LN_STEPS * (NG - 1))
                dve.wait_ge(h2_done, GB * (NG - 1))
                dve.wait_ge(bn2_done, GB * (NG - 1) + b1)
                dve.tensor_tensor(t[SUM], m0, m1, ALU.add).then_inc(ln2_last, 1)
                dve.tensor_tensor(t[DIFF], m0, m1, ALU.subtract).then_inc(ln2_last, 1)
                dve.tensor_tensor(t[SQ], q0, q1, ALU.add).then_inc(ln2_last, 1)
                dve.wait_ge(ln2_last, before + 2)
                dve.scalar_tensor_tensor(out=t[VAR_BETWEEN], in0=t[DIFF], scalar=0.25, in1=t[DIFF],
                                         op0=ALU.mult, op1=ALU.mult).then_inc(ln2_last, 1)
                dve.tensor_scalar(t[NEG_MEAN], t[SUM], -0.5, None, ALU.mult).then_inc(ln2_last, 1)
                dve.wait_ge(ln2_last, before + 4)
                dve.tensor_scalar(t[VAR_BETWEEN], t[VAR_BETWEEN], EPS_LN, None, ALU.add).then_inc(ln2_last, 1)
                dve.wait_ge(ln2_last, before + 6)
                dve.scalar_tensor_tensor(out=t[VAR], in0=t[SQ], scalar=1.0 / D, in1=t[VAR_BETWEEN],
                                         op0=ALU.mult, op1=ALU.add).then_inc(ln2_last, 1)

            def h2_lo(g, b):
                dve.wait_ge(h2_hi, GB * g + b + 1)
                dve.tensor_tensor(h2[1][:, b], h2f[:, b], part(h2[0][:, b]), ALU.subtract).then_inc(h2_split_dve, 1)

            def output(g, b, n):
                dve.wait_ge(l1_done, GB * g + b + 1)
                dve.wait_ge(x2b_ready, GB * g + b + 1)
                dve.tensor_tensor(x_out[:, b], bank(n), x_out[:, b], ALU.add).then_inc(drained, 1)

            def iteration(i, before=True, after=True):
                n = 0
                hi = first_hi(i)
                for a in range(C):
                    for l in range(2):
                        hi = hi + 1
                        lo(y[1][:, a, :, l], bank(n).rearrange("p (b m) -> p b m", b=GB), y[0][:, a, :, l], hi)\
                            .then_inc(drained, 1)
                        n += 1
                        if not before and G_USES - C <= n < G_USES:
                            factor_lo(2 * (n - G_USES + C))
                            factor_lo(2 * (n - G_USES + C) + 1)
                        if before and n == 1:
                            mask_g(i - 1)
                        if before and n == 2:
                            row_factors(i - 1)
                        if before and n == 4:
                            combine(i - 1)
                        if after and n == (6 if before else G_USES):
                            x_stats(i + 1)
                        if before and n == 6:
                            kt_lo(i - 1)
                if before:
                    residual(i - 1, n, first_use(i) + n)
                else:
                    for c in range(C):
                        hi += 1
                        lo(MT[1][:, c], bank(n + c), MT[0][:, c], hi).then_inc(drained, 1)
                n += GB
                if not after:
                    last_chain(i, n, hi)
                    return
                for b in range(GB):
                    hi = hi + 1
                    lo(v[1][:, b], bank(n), v[0][:, b], hi).then_inc(drained, 1)
                    n += 1
                    hi = hi + 1
                    t_lo(b, n, hi).then_inc(drained, 1 if before or b < GB - 1 else 1 + GB)
                    n += 1
                    if b == 0:
                        dve.wait_ge(diag_ready, i + 1)
                        wait_for(dve, rn_step, RN_STEPS * i)
                        wait_for(dve, p_shifted, i)
                        dve.tensor_reduce(sq[:, :, :], diag, AX.X, ALU.add).then_inc(sq_ready, 1)
                        dve.wait_ge(sq_ready, 2 * i + 1)
                        dve.tensor_scalar(sqc[:, :], sq[:, :, 0], EPS * EPS, None, ALU.max).then_inc(sq_ready, 1)
                    if b == 2:
                        sum_s(i)
                if before:
                    for b in range(GB - 1):
                        output(i - 1, b, n + b)
                similarities(i)
                if before:
                    output(i - 1, GB - 1, n + GB - 1)
                mask_l(i)

            def sum_s(g):
                dve.wait_ge(pt_done, g + 1)
                dve.tensor_tensor(A, p_ps[:, :, :, :], P_sb, ALU.add).then_inc(s_ready, 1)

            def last_chain(i, n, hi):
                select = diag_of[:, :, :].rearrange("p l m -> p (l m)").unsqueeze(1).to_broadcast([P, GB // 2, 2 * P])
                dve.wait_ge(rn_step, RN_STEPS * i)
                dve.wait_ge(p_shifted, i)
                for q in range(2):
                    half = slice(q * GB // 2, (q + 1) * GB // 2)
                    dve.wait_ge(p_copied, 2 * i + q + 1)
                    dve.tensor_tensor(diag[:, half].rearrange("p b l m -> p b (l m)"),
                                      P_sb[:, half].rearrange("p b l m -> p b (l m)"), select, ALU.mult)\
                       .then_inc(diag_ready, 1)
                    dve.wait_ge(diag_ready, i + q + 1)
                    dve.tensor_reduce(sq[:, half], diag[:, half], AX.X, ALU.add).then_inc(sq_ready, 1)
                dve.wait_ge(sq_ready, 2 * i + 2)
                dve.tensor_scalar(sqc[:, :], sq[:, :, 0], EPS * EPS, None, ALU.max).then_inc(sq_ready, 1)

                def v_lo(b):
                    lo(v[1][:, b], bank(n + b), v[0][:, b], hi + b + 1).then_inc(drained, 1)

                v_lo(0)
                sum_s(i)
                similarities(i)
                mask_l(i)
                mask_g(i)
                row_factors(i)
                for b in range(1, GB - 1):
                    v_lo(b)
                combine(i)
                v_lo(GB - 1)
                for b in range(GB):
                    output(i - 1, b, n + GB + b)
                    if b == 0:
                        kt_lo(i)

            def weight_lo(parts, raw, c, n):
                dve.wait_ge(w_hi, n)
                dve.tensor_tensor(parts[1][:, c], raw[:, c], part(parts[0][:, c]), ALU.subtract).then_inc(w_split, 1)

            def factor_lo(q):
                if q < C:
                    weight_lo(wv_parts, raw_v, q, 2 * C + q + 1)
                else:
                    dve.wait_ge(side_hi, q + 1)
                    dve.tensor_tensor(woT_parts[1][:, q - C], side[q - C], part(woT_parts[0][:, q - C]),
                                      ALU.subtract).then_inc(side_split, 1)

            def lw_lo(l, banks, hi_done, done):
                for c in range(C):
                    dve.wait_ge(hi_done, c + 1)
                    for a in range(c, C):
                        e = dve.scalar_tensor_tensor(
                            out=Lw[1][:, l, blk[a, c]], in0=banks[c][:, (a - c) * P:(a - c + 1) * P],
                            scalar=0.5 if a == c else 1.0, in1=part(Lw[0][:, l, blk[a, c]]),
                            op0=ALU.mult, op1=ALU.subtract)
                    e.then_inc(done, 1)

            for c in range(C):
                weight_lo(wl_parts, raw_l, c, c + 1)
            for c in range(C):
                weight_lo(wg_parts, raw_g, c, C + c + 1)
            x_stats(0)
            lw_lo(0, [bank(c) for c in range(C)], hi_ready, drained)
            dve.wait_ge(ident_ready, 4)
            dve.wait_ge(consts_loaded, 16 * 4)
            dve.tensor_tensor(mask[:, :], adj_sb[:, :], off_diag[:, :], ALU.mult)
            dve.tensor_tensor(adj2[:, :], adj_sb[:, :], adj_sb[:, :], ALU.mult).then_inc(a2_step, 1)
            dve.wait_ge(exp_gate, 2)
            dve.tensor_scalar(w_l, egate, 1.0, None, ALU.add).then_inc(scalars, 1)
            dve.tensor_tensor(sig2, sig, sig, ALU.mult).then_inc(scalars, 1)
            dve.wait_ge(scalars, 2)
            dve.reciprocal(w_l, w_l).then_inc(scalars, 1)
            dve.reciprocal(inv_sig2, sig2).then_inc(scalars, 1)
            dve.wait_ge(scalars, 4)
            dve.tensor_scalar(w_g, w_l, -1.0, 1.0, ALU.mult, ALU.add).then_inc(scalars, 1)
            dve.wait_ge(scalars, 5)
            for b in range(GB):
                dve.tensor_copy(w8[:, b], scal[:, 2:4]).then_inc(scalars, 1)
            lw_lo(1, side, side_hi, side_split)
            for b in range(GB):
                t_lo(b, SETUP + b, SETUP + b + 1).then_inc(drained, 1)
            dve.wait_ge(a2_hi, 1)
            dve.tensor_tensor(A2[1][:, :], adj2[:, :], part(A2[0][:, :]), ALU.subtract).then_inc(a2_step, 1)

            iteration(0, before=False)
            iteration(1)
            with dve.Fori(2, NG - 1) as i:
                iteration(i)
            iteration(NG - 1, after=False)
            g = NG - 1
            residual(g, 0, first_use(g) + PER - GB, last=True)
            h2_lo(g, 0)
            for b in range(1, GB):
                h2_lo(g, b)
                output(g, b - 1, b - 1)
            output(g, GB - 1, GB - 1)

        @block.tensor
        def _(pe):
            def free(use):
                wait_for(pe, drained, use - BANKS + 1)

            def transposes_h(g, b, n, use):
                pe.wait_ge(h_ready, GB * g + b + 1)
                free(use)
                for c in range(C):
                    mm = pe.transpose(bank(n)[:, c * P:(c + 1) * P], h[:, b, c * P:(c + 1) * P], ident[:, :])
                mm.then_inc(t_done, 1)

            def product(out, terms):
                for k, (lhsT, rhs) in enumerate(terms):
                    mm = pe.matmul(out, lhsT, rhs, start=(k == 0), stop=(k == len(terms) - 1))
                return mm

            def y_block(a, l, n, use):
                free(use)
                product(bank(n), [t for c in range(a + 1) for t in passes(
                    [w[:, l, blk[a, c]] for w in Lw],
                    [w[:, c].rearrange("p b m -> p (b m)") for w in hT])]).then_inc(g_done, 1)

            def transposes_K(g):
                pe.wait_ge(k_ready, g + 1)
                for b in range(GB):
                    mm = pe.transpose(kt_ps[:, b], K[:, b], ident[:, :])
                mm.then_inc(kt_done, 1)

            def k_v(g, b, n, use):
                free(use)
                product(bank(n), passes([w[:, b] for w in KT], [w[:, b] for w in v])).then_inc(kv_done, 1)

            def layer1(g, b, n, use, last=False):
                if last:
                    pe.wait_ge(h2_split_dve, b + 1)
                else:
                    pe.wait_ge(h2_split, GB * g + b + 1)
                free(use)
                product(bank(n), passes([w[:, :] for w in A2], [w[:, b] for w in h2])).then_inc(l1_done, 1)

            def transposes_rn(g):
                pe.wait_ge(rn_step, RN_STEPS * (g + 1))
                for b in range(GB):
                    mm = pe.transpose(r_ps[:, b], rn[:, b, 0:1].to_broadcast([P, P]), ident[:, :])
                mm.then_inc(r_done, 1)

            def iteration(i, before=True, after=True):
                n, use = 0, first_use(i)
                for a in range(C):
                    for l in range(2):
                        y_block(a, l, n, use + n)
                        n += 1
                        if before and n == G_USES - 1:
                            transposes_K(i - 1)
                        if not before and n == 1:
                            pe.wait_ge(side_split, C)
                if before:
                    pe.wait_ge(kt_split, i)
                    for b in range(GB):
                        k_v(i - 1, b, n + b, use + n + b)
                else:
                    pe.wait_ge(w_split, 3 * C)
                    pe.wait_ge(side_split, 2 * C)
                    for c in range(C):
                        free(use + n + c)
                        product(bank(n + c), [t for e in range(C) for t in passes(
                            [w[:, e, c * P:(c + 1) * P] for w in wv_parts], [w[:, e] for w in woT_parts])])\
                            .then_inc(setup_mm, 1)
                n += GB
                pe.wait_ge(drained, use + G_USES)
                for b in range(GB):
                    product(p_ps[:, b].rearrange("p l m -> p (l m)"), [t for a in range(C) for t in passes(
                        [w[:, a, b] for w in hT],
                        [w[:, a, b].rearrange("p l m -> p (l m)") for w in y])]).then_inc(p_done, 1)
                if not before:
                    pe.wait_ge(drained, use + G_USES + C)
                for b in range(GB):
                    free(use + n)
                    product(bank(n), [t for c in range(C) for t in passes(
                        [w[:, c, b] for w in hT], [w[:, c] for w in MT])]).then_inc(v_done, 1)
                    n += 1
                    if b == (2 if after else 0):
                        pe.wait_ge(p_shifted, i + 1)
                        for k in range(2 * GB):
                            mm = pe.transpose(p_ps[:, k // 2, k % 2], P_sb[:, k // 2, k % 2], ident[:, :])
                        mm.then_inc(pt_done, 1)
                        if not after:
                            transposes_rn(i)
                    if after:
                        transposes_h(i + 1, b, n, use + n)
                        n += 1
                if after:
                    transposes_rn(i)
                if before:
                    for b in range(GB):
                        if not after and b == GB // 2:
                            transposes_K(i)
                        layer1(i - 1, b, n + b, use + n + b)

            rows = [bank(c) for c in range(C)], side
            for l, parts in enumerate((wl_parts, wg_parts)):
                for e in range(C):
                    pe.wait_ge(w_split, C * l + e + 1)
                    for c in range(C):
                        for k, (lhsT, rhs) in enumerate(passes([w[:, e, c * P:(c + 1) * P] for w in parts],
                                                               [w[:, e, c * P:D] for w in parts])):
                            mm = pe.matmul(rows[l][c][:, 0:D - c * P], lhsT, rhs,
                                           start=(e == 0 and k == 0), stop=(e == C - 1 and k == 2))
                        if e == C - 1:
                            mm.then_inc(setup_mm, 1)
            pe.wait_ge(ident_ready, 4)
            for b in range(GB):
                transposes_h(0, b, SETUP + b, SETUP + b)
            pe.wait_ge(w_loaded["o"], 16)
            for c in range(C):
                pe.wait_ge(side_split, c + 1)
                for q in range(C):
                    mm = pe.transpose(side[c][:, q * P:(q + 1) * P], raw_o[:, q, c * P:(c + 1) * P], ident[:, :])
                mm.then_inc(setup_mm, 1)
            pe.wait_ge(drained, SETUP + GB)

            iteration(0, before=False)
            pe.wait_ge(a2_step, 2)
            iteration(1)
            with pe.Fori(2, NG - 1) as i:
                iteration(i)
            iteration(NG - 1, after=False)
            g = NG - 1
            use = first_use(g) + PER - GB
            pe.wait_ge(kt_split, NG)
            for b in range(GB):
                k_v(g, b, b, use + b)
            for b in range(GB):
                layer1(g, b, b, use + GB + b, last=True)


_INS = ["x", "adj", "L0_gnn_W_lang", "L0_gnn_W_grav", "L0_gnn_W_V", "L0_gnn_W_O",
        "L0_gnn_gate_logit", "L0_gnn_log_sigma", "L1_gnn_bias"]


def kernel(**inputs):
    import numpy as np
    import concourse.bacc as bacc
    from concourse.bass_utils import run_bass_kernel_spmd

    nc = bacc.Bacc("TRN2", target_bir_lowering=False, num_devices=1)
    arrays, args = {}, []
    for name in _INS:
        a = np.ascontiguousarray(inputs[name])
        if a.ndim == 0:
            a = a.reshape(1)
        arrays[f"in_{name}"] = a
        args.append(nc.dram_tensor(f"in_{name}", a.shape, mybir.dt.from_np(a.dtype), kind="ExternalInput").ap())
    out = nc.dram_tensor("out", arrays["in_x"].shape, F32, kind="ExternalOutput").ap()
    gnn_pair(nc, *args, out)
    r = run_bass_kernel_spmd(nc, [arrays], core_ids=[0])
    return r.results[0]["out"]
```
